# Optimizing a Trainium2 kernel written in Bass

```python
import numpy as np
import jax
import jax.numpy as jnp

def _softmax(x, axis=-1):
    return jax.nn.softmax(x, axis=axis)

def _gelu(x):
    return jax.nn.gelu(x, approximate=True)

def _silu(x):
    return jax.nn.silu(x)

def _sigmoid(x):
    return jax.nn.sigmoid(x)

def _layernorm(x, axis=-1, eps=1e-05):
    m = jnp.mean(x, axis=axis, keepdims=True)
    v = jnp.var(x, axis=axis, keepdims=True)
    return (x - m) / jnp.sqrt(v + eps)

def _scatter_add(tgt, idx, src, axis=0):
    return tgt.at[idx].add(src)

def _segment_sum(src, seg, n):
    return jax.ops.segment_sum(src, seg, n)
kernel_name = 'mk_xattn_ffn_d1_seqx_r4_8eb517'

def setup_inputs(seed: int=0):
    np.random.seed(seed)
    _w = jnp.asarray

    def _rec_inputs():
        import jax
        import jax.numpy as jnp
        _rk = jax.random.key(seed)
        x = 7.22e-05 + 1 * jax.random.normal(jax.random.fold_in(_rk, 1), (16, 256, 256), jnp.float32)
        _lenS = 256 - jax.random.randint(jax.random.fold_in(_rk, 7), (16,), 0, max(1, 256 // 4) + 1, jnp.int32)
        _lenS2 = 256 - jax.random.randint(jax.random.fold_in(_rk, 8), (16,), 0, max(1, 256 // 4) + 1, jnp.int32)
        _ctx_1024P = jax.random.normal(jax.random.fold_in(_rk, 11), (16, 16, 256), jnp.float32)
        _ctx_1024c = jax.random.dirichlet(jax.random.fold_in(_rk, 511), 0.3 * jnp.ones((16,), jnp.float32), (16, 256))
        _ctx_1024t = jnp.einsum('bsk,bkd->bsd', _ctx_1024c, _ctx_1024P)
        _ctx_1024t = _ctx_1024t * jax.lax.rsqrt(jnp.mean(jnp.square(_ctx_1024t)) + 1e-12) * 0.953939
        ctx_1024 = 4.13588e-05 + 0.999923 * (_ctx_1024t + 0.3 * jax.random.normal(jax.random.fold_in(_rk, 611), (16, 256, 256), jnp.float32))
        return (x, ctx_1024)
    x, ctx_1024 = _rec_inputs()

    def _L0_xattn_setup():
        import jax, jax.numpy as jnp
        import numpy as np
        HEADS = 8
        DIM_HEAD = 64
        key = jax.random.key(seed)
        ks = jax.random.split(key, 9)
        B, N1, N2, D = (4, 512, 512, 256)
        inner = HEADS * DIM_HEAD
        s_in = 1.0 / np.sqrt(D)
        s_inner = 1.0 / np.sqrt(inner)
        return {'x1': jax.random.normal(ks[0], (B, N1, D), jnp.float32), 'x2': jax.random.normal(ks[1], (B, N2, D), jnp.float32), 'Wq1': jax.random.normal(ks[2], (D, inner), jnp.float32) * s_in, 'Wk1': jax.random.normal(ks[3], (D, inner), jnp.float32) * s_in, 'Wv1': jax.random.normal(ks[4], (D, inner), jnp.float32) * s_in, 'Wk2': jax.random.normal(ks[5], (D, inner), jnp.float32) * s_in, 'Wv2': jax.random.normal(ks[6], (D, inner), jnp.float32) * s_in, 'Wo': jax.random.normal(ks[7], (inner, D), jnp.float32) * s_inner, 'bo': jnp.zeros((D,), jnp.float32)}
    _L0_xattn_all = _L0_xattn_setup()
    _L0_xattn_in = {k: v for k, v in _L0_xattn_all.items() if k in ('Wq1', 'Wk1', 'Wv1', 'Wk2', 'Wv2', 'Wo', 'bo')}
    del _L0_xattn_all

    def _L0_ffn_setup():
        import jax, jax.numpy as jnp
        import numpy as np
        D_MODEL = 256
        EXPERT_DIM = 512
        N_EXPERTS = 8
        LN_EPS = 1e-05

        def _bit_quant(W):
            scale = jnp.clip(jnp.mean(jnp.abs(W), axis=-1, keepdims=True), 1e-05, None)
            w_q = jnp.clip(jnp.round(W / scale), -1.0, 1.0) * scale
            return W + jax.lax.stop_gradient(w_q - W)
        key = jax.random.key(seed)
        ks = jax.random.split(key, 7)
        x = jax.random.normal(ks[0], (4, 512, D_MODEL), dtype=jnp.float32)
        shared_w1 = jax.random.normal(ks[1], (EXPERT_DIM, D_MODEL), dtype=jnp.float32) / np.sqrt(EXPERT_DIM)
        shared_w2 = jax.random.normal(ks[2], (D_MODEL, EXPERT_DIM), dtype=jnp.float32) / np.sqrt(D_MODEL)
        expert_w1 = jax.random.normal(ks[3], (N_EXPERTS, EXPERT_DIM, D_MODEL), dtype=jnp.float32) / np.sqrt(EXPERT_DIM)
        expert_w2 = jax.random.normal(ks[4], (N_EXPERTS, D_MODEL, EXPERT_DIM), dtype=jnp.float32) / np.sqrt(D_MODEL)
        router_w = 0.02 * jax.random.normal(ks[5], (N_EXPERTS, D_MODEL), dtype=jnp.float32)
        ln_gamma = jnp.ones((D_MODEL,), dtype=jnp.float32)
        ln_beta = jnp.zeros((D_MODEL,), dtype=jnp.float32)
        return {'x': x, 'shared_w1': shared_w1, 'shared_w2': shared_w2, 'expert_w1': expert_w1, 'expert_w2': expert_w2, 'router_w': router_w, 'ln_gamma': ln_gamma, 'ln_beta': ln_beta}
    _L0_ffn_all = _L0_ffn_setup()
    _L0_ffn_in = {k: v for k, v in _L0_ffn_all.items() if k in ('shared_w1', 'shared_w2', 'expert_w1', 'expert_w2', 'router_w', 'ln_gamma', 'ln_beta')}
    del _L0_ffn_all
    return {'x': x, 'ctx_1024': ctx_1024, 'L0_xattn_Wq1': _L0_xattn_in['Wq1'], 'L0_xattn_Wk1': _L0_xattn_in['Wk1'], 'L0_xattn_Wv1': _L0_xattn_in['Wv1'], 'L0_xattn_Wk2': _L0_xattn_in['Wk2'], 'L0_xattn_Wv2': _L0_xattn_in['Wv2'], 'L0_xattn_Wo': _L0_xattn_in['Wo'], 'L0_xattn_bo': _L0_xattn_in['bo'], 'L0_ffn_shared_w1': _L0_ffn_in['shared_w1'], 'L0_ffn_shared_w2': _L0_ffn_in['shared_w2'], 'L0_ffn_expert_w1': _L0_ffn_in['expert_w1'], 'L0_ffn_expert_w2': _L0_ffn_in['expert_w2'], 'L0_ffn_router_w': _L0_ffn_in['router_w'], 'L0_ffn_ln_gamma': _L0_ffn_in['ln_gamma'], 'L0_ffn_ln_beta': _L0_ffn_in['ln_beta']}

def reference(x, ctx_1024, L0_xattn_Wq1, L0_xattn_Wk1, L0_xattn_Wv1, L0_xattn_Wk2, L0_xattn_Wv2, L0_xattn_Wo, L0_xattn_bo, L0_ffn_shared_w1, L0_ffn_shared_w2, L0_ffn_expert_w1, L0_ffn_expert_w2, L0_ffn_router_w, L0_ffn_ln_gamma, L0_ffn_ln_beta):
    import jax
    import jax.numpy as jnp

    def _L0_xattn_ref(x1, x2, Wq1, Wk1, Wv1, Wk2, Wv2, Wo, bo):
        import jax, jax.numpy as jnp
        import numpy as np
        HEADS = 8
        DIM_HEAD = 64
        h, d = (HEADS, DIM_HEAD)
        scale = d ** (-0.5)
        B, N1, _ = x1.shape
        N2 = x2.shape[1]

        def split_heads(t, n):
            return t.reshape(B, n, h, d)
        q1 = split_heads(x1 @ Wq1, N1)
        k1 = split_heads(x1 @ Wk1, N1)
        v1 = split_heads(x1 @ Wv1, N1)
        k2 = split_heads(x2 @ Wk2, N2)
        v2 = split_heads(x2 @ Wv2, N2)
        k = jnp.concatenate([k1, k2], axis=1)
        v = jnp.concatenate([v1, v2], axis=1)
        sim = jnp.einsum('bihd,bjhd->bhij', q1.astype(jnp.float32), k.astype(jnp.float32)) * scale
        attn = jax.nn.softmax(sim, axis=-1)
        out = jnp.einsum('bhij,bjhd->bihd', attn, v)
        out = out.reshape(B, N1, h * d)
        return out @ Wo + bo

    def _L0_ffn_ref(x, shared_w1, shared_w2, expert_w1, expert_w2, router_w, ln_gamma, ln_beta):
        import jax, jax.numpy as jnp
        import numpy as np
        D_MODEL = 256
        EXPERT_DIM = 512
        N_EXPERTS = 8
        LN_EPS = 1e-05

        def _bit_quant(W):
            scale = jnp.clip(jnp.mean(jnp.abs(W), axis=-1, keepdims=True), 1e-05, None)
            w_q = jnp.clip(jnp.round(W / scale), -1.0, 1.0) * scale
            return W + jax.lax.stop_gradient(w_q - W)
        mu = jnp.mean(x, axis=-1, keepdims=True)
        var = jnp.mean(jnp.square(x - mu), axis=-1, keepdims=True)
        h = (x - mu) / jnp.sqrt(var + LN_EPS) * ln_gamma + ln_beta
        sw1, sw2 = (_bit_quant(shared_w1), _bit_quant(shared_w2))
        shared_out = jax.nn.silu(jnp.einsum('btd,fd->btf', h, sw1)) @ sw2.T
        probs = jax.nn.softmax(h @ router_w.T, axis=-1)
        top_prob = jnp.max(probs, axis=-1)
        top_idx = jnp.argmax(probs, axis=-1)
        ew1, ew2 = (_bit_quant(expert_w1), _bit_quant(expert_w2))
        h1 = jax.nn.silu(jnp.einsum('btd,efd->ebtf', h, ew1))
        eo = jnp.einsum('ebtf,edf->ebtd', h1, ew2)
        gate = jax.nn.one_hot(top_idx, N_EXPERTS, dtype=h.dtype) * top_prob[..., None]
        routed_out = jnp.einsum('ebtd,bte->btd', eo, gate)
        return shared_out + routed_out
    x = x + _L0_xattn_ref(_layernorm(x, axis=-1), ctx_1024, L0_xattn_Wq1, L0_xattn_Wk1, L0_xattn_Wv1, L0_xattn_Wk2, L0_xattn_Wv2, L0_xattn_Wo, L0_xattn_bo)
    x = x + _L0_ffn_ref(_layernorm(x, axis=-1), L0_ffn_shared_w1, L0_ffn_shared_w2, L0_ffn_expert_w1, L0_ffn_expert_w2, L0_ffn_router_w, L0_ffn_ln_gamma, L0_ffn_ln_beta)
    return x

_drawn_inputs = setup_inputs


def setup_inputs(seed=0):
    import zlib

    import numpy as np

    out = dict(_drawn_inputs(seed))
    spreads = {'L0_xattn_bo': (0.0, 0.1), 'L0_ffn_ln_gamma': (1.0, 0.2), 'L0_ffn_ln_beta': (0.0, 0.296)}
    factors = {}
    for name, (base, spread) in spreads.items():
        noise = np.random.default_rng([zlib.crc32(name.encode()), seed]).standard_normal(out[name].shape)
        drawn = base * np.exp(spread * noise) if base else spread * noise
        out[name] = jnp.asarray(drawn.astype(out[name].dtype))
    for name, factor in factors.items():
        out[name] = (out[name] * factor).astype(out[name].dtype)
    return out
```

```python
from contextlib import ExitStack

import concourse.bass as bass
from concourse import mybir

F32 = mybir.dt.float32
F16 = mybir.dt.float16
F32R = mybir.dt.float32r
I32 = mybir.dt.int32
U32 = mybir.dt.uint32
ALU = mybir.AluOpType
ACT = mybir.ActivationFunctionType
AX = mybir.AxisListType

P = 128
B, T, D = 16, 256, 256
HEADS, DH = 8, 64
INNER = HEADS * DH
KEYS = 2 * T
DC = D // P
IC = INNER // P
TB = T // P
KB = KEYS // P
UNITS = TB * HEADS
E, FW = 8, 512
FC = FW // P
EPS = 1e-5
QSCALE = DH ** -0.5
HSCALE = 16.0
RSCALE = 64.0
TILES = B * TB
SLOTS = TILES + E
RING = 4
ABSENT = 8192

FC_CTX, V2, FC_X, V3, Q0, Q1, K0, K1, K2, K3, V0, V1, QUANT = range(13)
FRONT_AT = {0: FC_CTX, 2: V2, 3: FC_X, 4: V3, 5: Q0, 6: Q1, 7: K0, 8: K1, 9: K2, 10: K3, 11: V0, 12: V1, 14: QUANT}
FRONT = 13
SPLIT = 12
OT0, WO0, OT1, WO1, HT, ROUTER, UP0, UP1, DOWN = range(9)
TAIL_AT = {0: OT0, 1: WO0, 3: OT1, 4: WO1, 7: HT, 9: ROUTER, 10: UP0, 11: UP1, 14: DOWN}
TAIL = 9
SHARED_Q = 2
PREP = 3


def xattn_ffn(nc, x, ctx_in, wq1, wk1, wv1, wk2, wv2, wo, bo, sw1, sw2, ew1, ew2, router_w, gamma, beta, out):
    rows = nc.dram_tensor("rows", [B * T, 2 * D], F32, kind="Internal").ap()
    with ExitStack() as ctx:
        def sb(name, shape, dt):
            return ctx.enter_context(nc.sbuf_tensor(name, shape, dt))

        def bank(name):
            return ctx.enter_context(nc.psum_tensor(name, [P, 512], F32))

        def sem(name):
            return ctx.enter_context(nc.semaphore(name))

        ident = sb("ident", [P, P], F32)
        ident16 = sb("ident16", [P, P], F16)
        ones = sb("ones", [P, P], F32)
        below16 = sb("below16", [P, P], F16)
        ones16 = sb("ones16", [P, P], F16)
        minus_half = sb("minus_half", [P, TB], F32)
        WQ, WK1, WV1, WK2, WV2 = range(5)
        w_hi = sb("w_hi", [P, 5, DC, INNER], F32R)
        w_lo = sb("w_lo", [P, 5, DC, INNER], F32R)
        wo_hi = sb("wo_hi", [P, IC, D], F32R)
        wo_lo = sb("wo_lo", [P, IC, D], F32R)
        up16 = sb("up16", [P, E + 1, DC, FW], F16)
        down16 = sb("down16", [P, E + 1, FC, D], F16)
        up_scale = sb("up_scale", [P, E + 1, FC], F32)
        down_scale = sb("down_scale", [P, E + 1, DC], F32)
        half_up = sb("half_up", [P, FC], F32)
        shared_row = sb("shared_row", [P, D], F32)
        gb = sb("gb", [P, 2, DC], F32)
        bo_row = sb("bo_row", [P, D], F32)
        small = sb("small", [P, D], F32)
        rw_hi = sb("rw_hi", [P, DC, E], F16)
        rw_lo = sb("rw_lo", [P, DC, E], F16)
        x_in = sb("x_in", [P, TB, D], F32)
        c_in = sb("c_in", [P, TB, D], F32)
        x1 = sb("x1", [P, TB, D], F32)
        st1 = sb("st1", [P, TB, 6], F32)
        mv1 = sb("mv1", [P, TB, 2], F32)
        ve1 = sb("ve1", [P, TB], F32)
        rs1 = sb("rs1", [P, TB], F32)
        xt_hi = sb("xt_hi", [P, DC, KEYS], F32R)
        xt_lo = sb("xt_lo", [P, DC, KEYS], F32R)
        q_stage = [sb(f"q_stage{i}", [P, 2, 2, T], F16) for i in range(2)]
        k_stage = [sb(f"k_stage{i}", [P, 2, KEYS], F16) for i in range(2)]
        q_st = [sb(f"q_st{i}", [P, HEADS, 2, T], F16) for i in range(2)]
        k_st = [sb(f"k_st{i}", [P, HEADS, KEYS], F16) for i in range(2)]
        v_st = [sb(f"v_st{i}", [P, 2, KB, HEADS, DH], F16) for i in range(2)]
        pause = sb("pause", [P, 1], F32)
        w_raw = sb("w_raw", [P, 1024], F32)
        w_abs = sb("w_abs", [P, FC], F32)
        w_half = sb("w_half", [P, 2, FC], F32)
        above = sb("above", [P, 1024], F16)
        under = sb("under", [P, 1024], F16)
        probs = [sb(f"probs{i}", [P, KEYS], F32) for i in range(2)]
        neg_max = sb("neg_max", [P, 4], F32)
        pt_hi = [sb(f"pt_hi{i}", [P, KB, P], F16) for i in range(2)]
        pt_lo = [sb(f"pt_lo{i}", [P, KB, P], F16) for i in range(2)]
        sums = sb("sums", [P, UNITS], F32)
        inv_sum = sb("inv_sum", [P, 4], F32)
        o_sb = sb("o_sb", [P, TB, INNER], F32)
        ot_hi = sb("ot_hi", [P, IC, P], F32R)
        ot_lo = sb("ot_lo", [P, IC, P], F32R)
        xb = sb("xb", [P, TB, D], F32)
        x2 = sb("x2", [P, TB, D], F32)
        st2 = sb("st2", [P, TB, 6], F32)
        mv2 = sb("mv2", [P, TB, 2], F32)
        ve2 = sb("ve2", [P, TB], F32)
        rs2 = sb("rs2", [P, TB], F32)
        row = sb("row", [P, TB, 2 * D], F32)
        ht = sb("ht", [P, DC, T], F32)
        ht_hi = sb("ht_hi", [P, DC, T], F16)
        ht_lo = sb("ht_lo", [P, DC, T], F16)
        logits = sb("logits", [P, TILES, E], F32)
        th = sb("th", [P, 2, T], F32)
        gate = [sb(f"gate{i}", [P, 2, T], F32) for i in range(2)]
        g_hi = sb("g_hi", [P, FC, T], F16)
        g_lo = sb("g_lo", [P, FC, T], F16)

        S = [bank("S0"), bank("S1")]
        PT = [bank("PT0"), bank("PT1")]
        O = bank("O")
        FB = [bank("FB0"), bank("FB1")]
        TBK = bank("TBK")

        const_ready = sem("const_ready")
        weights_in = sem("weights_in")
        small_in = sem("small_in")
        rw_in = sem("rw_in")
        gb_in = sem("gb_in")
        w_hi_ready = sem("w_hi_ready")
        w_lo_ready = sem("w_lo_ready")
        prep_full = sem("prep_full")
        prep_free = sem("prep_free")
        rw_hi_ready = sem("rw_hi_ready")
        diag_ready = sem("diag_ready")
        x_loaded = sem("x_loaded")
        c_loaded = sem("c_loaded")
        stats1 = sem("stats1")
        var1 = sem("var1")
        ve1_ready = sem("ve1_ready")
        rs1_ready = sem("rs1_ready")
        x1_ready = sem("x1_ready")
        f_full = sem("f_full")
        f_hi = sem("f_hi")
        f_lo = sem("f_lo")
        q_stacked = [sem("q_stacked0"), sem("q_stacked1")]
        k_stacked = [sem("k_stacked0"), sem("k_stacked1")]
        raw_loaded = sem("raw_loaded")
        abs_ready = sem("abs_ready")
        scale_ready = sem("scale_ready")
        half_ready = sem("half_ready")
        half_up_ready = sem("half_up_ready")
        sign_ready = sem("sign_ready")
        tern_ready = sem("tern_ready")
        tern_moved = sem("tern_moved")
        scores_ready = sem("scores_ready")
        max_ready = sem("max_ready")
        probs_ready = sem("probs_ready")
        pt_ready = sem("pt_ready")
        pt_hi_ready = sem("pt_hi_ready")
        pt_lo_ready = sem("pt_lo_ready")
        pv_done = sem("pv_done")
        inv_ready = sem("inv_ready")
        normed = sem("normed")
        t_full = sem("t_full")
        ot_lo_ready = sem("ot_lo_ready")
        ht_ready = sem("ht_ready")
        logits_ready = sem("logits_ready")
        ot_hi_ready = sem("ot_hi_ready")
        xr_loaded = sem("xr_loaded")
        xb_ready = sem("xb_ready")
        x2_ready = sem("x2_ready")
        stats2 = sem("stats2")
        var2 = sem("var2")
        ve2_ready = sem("ve2_ready")
        rs2_ready = sem("rs2_ready")
        hn_ready = sem("hn_ready")
        h_hi_ready = sem("h_hi_ready")
        h_lo_ready = sem("h_lo_ready")
        th_ready = sem("th_ready")
        gate_ready = sem("gate_ready")
        gated = sem("gated")
        g_hi_ready = sem("g_hi_ready")
        g_lo_ready = sem("g_lo_ready")
        shared_ready = sem("shared_ready")
        r_ready = sem("r_ready")
        rows_stored = sem("rows_stored")
        iota_ready = sem("iota_ready")
        dve_step = sem("dve_step")
        exps_ready = sem("exps_ready")
        onehot_ready = sem("onehot_ready")
        ranks_ready = sem("ranks_ready")
        maps_ready = sem("maps_ready")
        slots_ready = sem("slots_ready")
        table_ready = sem("table_ready")
        dmat_ready = sem("dmat_ready")
        rowscale_full = sem("rowscale_full")
        rowscale_free = sem("rowscale_free")
        zeroed = sem("zeroed")
        gathered = [sem(f"gathered{i}") for i in range(RING)]
        e_ht_full = sem("e_ht_full")
        e_ht = sem("e_ht")
        e_ht_hi = sem("e_ht_hi")
        e_ht_lo = sem("e_ht_lo")
        e_up_full = sem("e_up_full")
        e_u = sem("e_u")
        e_th = sem("e_th")
        e_g = sem("e_g")
        e_g_hi = sem("e_g_hi")
        e_g_lo = sem("e_g_lo")
        e_down_full = sem("e_down_full")
        e_y = sem("e_y")
        e_out = sem("e_out")
        stored = [sem("stored0"), sem("stored1")]

        block = ctx.enter_context(nc.Block())

        def at_least(eng, s, value):
            if isinstance(value, int) and value <= 0:
                return
            eng.wait_ge(s, value)

        def slots(eng, body):
            for b in range(-1, 2):
                body(b, b % 2, (b + 1) // 2)
            with eng.Fori(1, B // 2 - 1) as i:
                body(i * 2, 0, i)
                body(i * 2 + 1, 1, i + 1)
            for b in range(B - 2, B + 1):
                body(b, b % 2, (b + 1) // 2)

        def is_static(b):
            return isinstance(b, int)

        def has_front(b):
            return not is_static(b) or b + 1 < B

        def has_attention(b):
            return not is_static(b) or 0 <= b < B

        def has_tail(b):
            return not is_static(b) or b >= 1

        def units_of(b):
            return range(UNITS)

        def quant_job(n):
            if is_static(n) and n < SHARED_Q:
                return n + 1
            return (n - SHARED_Q) * FRONT + SHARED_Q + QUANT + 1

        def split_product(o, pairs):
            terms = [t for (lh, ll, rh, rl) in pairs for t in ((lh, rh), (lh, rl), (ll, rh))]
            for n, (l, r) in enumerate(terms):
                mm = nc.tensor.matmul(o, l, r, start=(n == 0), stop=(n == len(terms) - 1))
            return mm

        x_v = x.rearrange("b (t p) d -> b p t d", p=P)
        c_v = ctx_in.rearrange("b (t p) d -> b p t d", p=P)
        rows_v = rows.rearrange("(b t p) d -> b p t d", p=P, t=TB)
        ew1_v = ew1.rearrange("e (c p) d -> e p c d", p=P)
        ew2_v = ew2.rearrange("e (c p) f -> e p c f", p=P)
        raw_up = w_raw[:, :].rearrange("p (c d) -> p c d", c=FC)
        raw_down = w_raw[:, :].rearrange("p (c f) -> p c f", c=DC)
        fb2 = [a[:, :].rearrange("p (c t) -> p c t", c=2) for a in FB]
        fb_heads = [a[:, :].rearrange("p (h d) -> p h d", h=HEADS) for a in FB]
        fb16 = [a[:, :].bitcast(F16) for a in FB]
        tb2 = TBK[:, :].rearrange("p (c t) -> p c t", c=2)
        landing = [k_st[0][:, 0:4, :], k_st[0][:, 4:8, :], k_st[1][:, 0:4, :], k_st[1][:, 4:8, :],
                   q_st[1][:, 0:4, :, :].rearrange("p h a t -> p h (a t)"), q_st[1][:, 4:8, :, :].rearrange("p h a t -> p h (a t)")]
        landing = [a.rearrange("p a b -> p (a b)").bitcast(F32) for a in landing]
        diag = probs[0][:, 0:2 * P].rearrange("p (c t) -> p c t", c=DC)

        score_e = probs[0][:, 0:TILES * E].rearrange("p (t e) -> p t e", e=E)
        hot = probs[0][:, TILES * E:2 * TILES * E].rearrange("p (t e) -> p t e", e=E)
        exps = probs[1][:, 0:TILES * E].rearrange("p (t e) -> p t e", e=E)
        incl = probs[1][:, TILES * E:2 * TILES * E].rearrange("p (t e) -> p t e", e=E)
        hot16 = g_hi[:, 0, :].rearrange("p (t e) -> p t e", e=E)
        counts = gate[0][:, 0, :].rearrange("p (t e) -> p t e", e=E)
        place = gate[0][:, 1, :].rearrange("p (t e) -> p t e", e=E)
        steps32 = gate[1][:, 0, :].rearrange("p (e t) -> p e t", e=E)
        flat = gate[1][:, 1, :]
        top, total, tiles_of, tile_end = flat[:, 0:32], flat[:, 32:40], flat[:, 40:48], flat[:, 48:56]
        base, dest, slot_tile, lane = flat[:, 56:64], flat[:, 64:96], flat[:, 96:128], flat[:, 128:160]
        prob, esum, one8 = flat[:, 160:192], flat[:, 192:224], flat[:, 224:232]
        desti = th[:, 0, 0:32].bitcast(I32)
        tilei = th[:, 0, 32:64].bitcast(I32)
        lanei = th[:, 0, 64:96].bitcast(I32)
        slot_prob = th[:, 0, 96:96 + SLOTS]
        slot_id = th[:, 0, 144:144 + SLOTS]
        slot_idx = th[:, 1, 0:SLOTS].bitcast(U32)
        tile_e = th[:, 1, 48:48 + SLOTS]
        tile_ei = th[:, 1, 96:96 + SLOTS].bitcast(I32)
        absent = th[:, 1, 144:144 + SLOTS]
        p_hi = g_hi[:, 1, 0:32]
        p_lo = g_hi[:, 1, 32:64]
        iota_lane = x_in[:, 0, 0:P]
        iota_tile = x_in[:, 0, P:P + SLOTS]
        iota_tiles128 = x_in[:, 1, 0:TILES]
        iota_tile1 = x_in[:, 1, 32:32 + TILES]
        iota_down = x_in[:, 1, 64:64 + E]
        iota_p = x_in[:, 1, 96:97]
        ones32 = x_in[:, 1, 128:128 + TILES]
        lane_hot = q_st[0][:, :, :, :].rearrange("p a h t -> p (a h t)").rearrange("p (t l) -> p t l", l=P)
        tile_hot = w_raw[:, :].bitcast(F16)[:, 0:TILES * SLOTS].rearrange("p (t a) -> p t a", a=SLOTS)
        map_ids = q_st[1][:, :, :, :].rearrange("p a h t -> p (a h t)")[:, 0:TILES * 2 * SLOTS]\
            .rearrange("p (t g a) -> p t g a", g=2, a=SLOTS)
        map_probs = v_st[0][:, :, :, :, :].rearrange("p a b h t -> p (a b h t)")[:, 0:TILES * 2 * SLOTS]\
            .rearrange("p (t g a) -> p t g a", g=2, a=SLOTS)
        diag_all = k_st[1][:, :, :].rearrange("p a b -> p (a b)").bitcast(F32)
        row_scales = k_st[0][:, :, :].rearrange("p a b -> p (a b)").bitcast(F32)\
            .rearrange("p (e d) -> p e d", e=E)
        g_rows = [row[:, 0, :], row[:, 1, :], probs[0][:, :], probs[1][:, :]]
        e_htf = [ht[:, :, 0:P], ht[:, :, P:2 * P]]
        e_hth = [ht_hi[:, :, 0:P], ht_hi[:, :, P:2 * P]]
        e_htl = [ht_lo[:, :, 0:P], ht_lo[:, :, P:2 * P]]
        e_up = [x1[:, 0:2, :].rearrange("p a b -> p (a b)"), x2[:, 0:2, :].rearrange("p a b -> p (a b)")]
        e_tanh = [xb[:, :, :].rearrange("p a b -> p (a b)"), c_in[:, :, :].rearrange("p a b -> p (a b)")]
        e_gate = [o_sb[:, 0, :], o_sb[:, 1, :]]
        e_gh = [k_stage[0][:, 0, :], k_stage[0][:, 1, :]]
        e_gl = [k_stage[1][:, 0, :], k_stage[1][:, 1, :]]
        e_yv = [w_raw[:, 0:D], w_raw[:, D:2 * D]]
        OE = [O[:, 0:D], FB[1][:, 0:D]]
        e_res = [w_raw[:, 2 * D:3 * D], w_raw[:, 3 * D:4 * D]]

        @block.sync
        def _(sp):
            sp.dma_start(x_in[:, :, :], x_v[0]).then_inc(x_loaded, 16)
            sp.dma_start(c_in[:, :, :], c_v[0]).then_inc(c_loaded, 16)
            for n, w in ((WV2, wv2), (WQ, wq1), (WK1, wk1), (WK2, wk2), (WV1, wv1)):
                sp.dma_start(landing[n].rearrange("p (c n) -> p c n", c=DC),
                             w.rearrange("(c p) n -> p c n", p=P)).then_inc(weights_in, 16)
            sp.dma_start(landing[5].rearrange("p (c n) -> p c n", c=IC),
                         wo.rearrange("(c p) n -> p c n", p=P)).then_inc(weights_in, 16)
            sp.dma_start(raw_up, sw1.rearrange("(c p) d -> p c d", p=P)).then_inc(raw_loaded, 16)
            sp.dma_start(small[0:E, :], router_w).then_inc(rw_in, 16)
            sp.dma_start(gb[:, 0, :], gamma.rearrange("(c p) -> p c", p=P), allow_slow_non_contiguous=True).then_inc(gb_in, 16)
            sp.dma_start(gb[:, 1, :], beta.rearrange("(c p) -> p c", p=P), allow_slow_non_contiguous=True).then_inc(gb_in, 16)
            sp.dma_start(xb[:, :, :], x_v[0]).then_inc(xr_loaded, 16)
            sp.wait_ge(tern_ready, 1)
            sp.dma_start(raw_down, sw2.rearrange("(c p) f -> p c f", p=P)).then_inc(raw_loaded, 16)
            sp.wait_ge(prep_full, 1)
            sp.dma_start(small[0:1, :], bo.rearrange("(a n) -> a n", a=1)).then_inc(small_in, 16)

            def body(b, par, e):
                f, t, fp = b + 1, b - 1, 1 - par
                if has_front(b):
                    at_least(sp, tern_ready, f + SHARED_Q)
                    src = (ew1_v if fp == 0 else ew2_v)[bass.ds(e, 1)].rearrange("e p c d -> p (e c) d")
                    sp.dma_start(raw_up if fp == 0 else raw_down, src).then_inc(raw_loaded, 16)
                    if not is_static(b) or f + 1 < B:
                        nb = bass.ds(f + 1, 1)
                        sp.wait_ge(f_full, f * FRONT + SHARED_Q + FC_CTX + 1)
                        sp.dma_start(c_in[:, :, :], c_v[nb].rearrange("b p t d -> p (b t) d")).then_inc(c_loaded, 16)
                        sp.wait_ge(x1_ready, f + 1)
                        sp.dma_start(x_in[:, :, :], x_v[nb].rearrange("b p t d -> p (b t) d")).then_inc(x_loaded, 16)
                    for s in range(2):
                        sp.wait_ge(f_lo, f * SPLIT + Q0 + s + 1)
                        for odd in range(2):
                            for half in range(2):
                                sp.dma_start(q_st[fp][half * DH:(half + 1) * DH, 4 * s + odd:4 * s + odd + 3:2, :, :],
                                             q_stage[s][odd * DH:(odd + 1) * DH, :, :, :]).then_inc(q_stacked[s], 16)
                    for c in range(IC):
                        sp.wait_ge(f_lo, f * SPLIT + K0 + c + 1)
                        for odd in range(2):
                            for half in range(2):
                                sp.dma_start(k_st[fp][half * DH:(half + 1) * DH, 2 * c + odd, :],
                                             k_stage[c % 2][odd * DH:(odd + 1) * DH, half, :])\
                                    .then_inc(k_stacked[c % 2], 16)
                if has_tail(b):
                    if not is_static(b) or t + 1 < B:
                        sp.wait_ge(x2_ready, t * 2 + 2)
                        sp.dma_start(xb[:, :, :], x_v[bass.ds(t + 1, 1)].rearrange("b p t d -> p (b t) d"))\
                            .then_inc(xr_loaded, 16)
                    sp.wait_ge(r_ready, t + 1)
                    sp.dma_start(rows_v[bass.ds(t, 1)].rearrange("b p t d -> p (b t) d"), row[:, :, :])\
                        .then_inc(rows_stored, 16)

            slots(sp, body)

        @block.gpsimd
        def _(pool):
            g = nc.gpsimd
            g.memset(ident[:, :], 0.0).then_inc(const_ready, 1)
            g.memset(ident16[:, :], 0.0).then_inc(const_ready, 1)
            g.memset(below16[:, :], 1.0).then_inc(const_ready, 1)
            g.memset(ones[:, :], 1.0).then_inc(const_ready, 1)
            g.memset(ones16[:, :], 1.0).then_inc(const_ready, 1)
            g.memset(minus_half[:, :], -0.5).then_inc(const_ready, 1)
            pool.wait_ge(const_ready, 6)
            for m in (ident, ident16):
                g.affine_select(out=m[:, :], in_=m[:, :], compare_op=ALU.not_equal, fill=1.0, base=0,
                                pattern=[[-1, P]], channel_multiplier=1).then_inc(const_ready, 1)
            g.affine_select(out=below16[:, :], in_=below16[:, :], compare_op=ALU.is_gt, fill=0.0, base=0,
                            pattern=[[1, P]], channel_multiplier=-1).then_inc(const_ready, 1)

            def body(b, par, e):
                f, t, fp = b + 1, b - 1, 1 - par
                if has_front(b):
                    pool.wait_ge(ve1_ready, f + 1)
                    g.tensor_tensor(rs1[:, :], ve1[:, :], minus_half[:, :], ALU.pow).then_inc(rs1_ready, 1)
                def ternary():
                    n = f + SHARED_Q
                    pool.wait_ge(sign_ready, n * 2 + 2)
                    g.tensor_tensor(above[:, :], above[:, :], under[:, :], ALU.subtract).then_inc(tern_ready, 1)

                if has_front(b) and not has_tail(b):
                    ternary()
                if has_tail(b):
                    pool.wait_ge(xr_loaded, (t + 1) * 16)
                    if is_static(b) and b == 1:
                        pool.wait_ge(prep_free, PREP)
                    g.tensor_tensor(xb[:, :, :], xb[:, :, :], bo_row[:, :].unsqueeze(1).broadcast_to([P, TB, D]),
                                    ALU.add).then_inc(xb_ready, 1)
                    pool.wait_ge(ve2_ready, t + 1)
                    g.tensor_tensor(rs2[:, :], ve2[:, :], minus_half[:, :], ALU.pow).then_inc(rs2_ready, 1)
                    pool.wait_ge(h_hi_ready, t + 1)
                    g.tensor_tensor(ht_lo[:, :, :], ht[:, :, :], ht_hi[:, :, :], ALU.subtract).then_inc(h_lo_ready, 1)
                    if has_front(b):
                        ternary()
                    for j in range(2):
                        pool.wait_ge(gate_ready, t * 2 + j + 1)
                        sc = up_scale[:, E, 2 * j:2 * j + 2].unsqueeze(2).broadcast_to([P, 2, T])
                        g.tensor_tensor(gate[j][:, :, :], gate[j][:, :, :], sc, ALU.mult).then_inc(gated, 1)
                        pool.wait_ge(g_hi_ready, t * 2 + j + 1)
                        g.tensor_tensor(g_lo[:, 2 * j:2 * j + 2, :], gate[j][:, :, :], g_hi[:, 2 * j:2 * j + 2, :],
                                        ALU.subtract).then_inc(g_lo_ready, 1)
                    pool.wait_ge(shared_ready, t + 1)
                    g.tensor_tensor(row[:, :, 0:D], row[:, :, 0:D], x2[:, :, :], ALU.add).then_inc(r_ready, 1)

            slots(pool, body)

            pool.wait_ge(rows_stored, 16 * B)
            g.iota(iota_lane, [[1, P]], base=0, channel_multiplier=0,
                   allow_small_or_imprecise_dtypes=True).then_inc(iota_ready, 1)
            g.iota(iota_tile, [[1, SLOTS]], base=0, channel_multiplier=0,
                   allow_small_or_imprecise_dtypes=True).then_inc(iota_ready, 1)
            g.iota(iota_tiles128, [[P, TILES]], base=0, channel_multiplier=0,
                   allow_small_or_imprecise_dtypes=True).then_inc(iota_ready, 1)
            g.iota(iota_tile1, [[1, TILES]], base=1, channel_multiplier=0,
                   allow_small_or_imprecise_dtypes=True).then_inc(iota_ready, 1)
            g.iota(iota_down, [[-1, E]], base=E, channel_multiplier=0,
                   allow_small_or_imprecise_dtypes=True).then_inc(iota_ready, 1)
            g.iota(iota_p, [[1, 1]], base=0, channel_multiplier=1,
                   allow_small_or_imprecise_dtypes=True).then_inc(iota_ready, 1)
            g.memset(ones32, 1.0).then_inc(iota_ready, 1)
            g.memset(row[:, :, :], 0.0).then_inc(zeroed, 1)
            pool.wait_ge(zeroed, 1)
            pool.wait_ge(table_ready, 1)

            def gather(a):
                if a >= RING:
                    pool.wait_ge(e_out, a - RING + 1)
                g.indirect_dma_start(out=g_rows[a % RING], out_offset=None, in_=rows,
                                     in_offset=bass.IndirectOffsetOnAxis(ap=slot_idx[:, a:a + 1], axis=0),
                                     bounds_check=B * T - 1, oob_is_err=False).then_inc(gathered[a % RING], 16)

            for a in range(RING):
                gather(a)
            for a in range(SLOTS):
                pool.wait_ge(e_y, a + 1)
                if a >= 2:
                    pool.wait_ge(stored[a % 2], 16 * (a // 2))
                g.tensor_tensor(e_res[a % 2], e_yv[a % 2], g_rows[a % RING][:, 0:D], ALU.add).then_inc(e_out, 1)
                pool.wait_ge(e_out, a + 1)
                g.indirect_dma_start(out=out, out_offset=bass.IndirectOffsetOnAxis(ap=slot_idx[:, a:a + 1], axis=0),
                                     in_=e_res[a % 2], in_offset=None,
                                     bounds_check=B * T - 1, oob_is_err=False).then_inc(stored[a % 2], 16)
                if a + RING < SLOTS:
                    gather(a + RING)
            for i in range(2):
                pool.wait_ge(stored[i], 16 * (SLOTS // 2))

        @block.scalar
        def _(act):
            a_ = nc.scalar.activation
            for n in range(5):
                act.wait_ge(weights_in, 16 * 6)
                a_(w_hi[:, n, :, :], landing[n].rearrange("p (c n) -> p c n", c=DC), ACT.Copy,
                   scale=QSCALE if n == WQ else 1.0).then_inc(w_hi_ready, 1)
            a_(wo_hi[:, :, :], landing[5].rearrange("p (c n) -> p c n", c=IC), ACT.Copy).then_inc(w_hi_ready, 1)

            def ternary_move(n, e, down, k):
                act.wait_ge(f_full, n[0])
                if down:
                    dst = down16[:, bass.ds(e, 1), :, :].rearrange("p a c d -> p (a c d)")
                else:
                    dst = up16[:, bass.ds(e, 1), :, :].rearrange("p a c f -> p (a c f)")
                a_(dst, fb16[k], ACT.Copy).then_inc(tern_moved, 1)

            ternary_move((1,), E, False, 1)
            act.wait_ge(prep_full, 1)
            tbr = TBK[:, 0:DC * E].rearrange("p (c e) -> p c e", c=DC)
            a_(rw_hi[:, :, :], tbr, ACT.Copy, scale=RSCALE).then_inc(rw_hi_ready, 1)
            ternary_move((2,), E, True, 1)
            act.wait_ge(prep_full, 2)
            a_(bo_row[:, :], TBK[:, 0:D], ACT.Copy).then_inc(prep_free, 1)
            act.wait_ge(prep_full, 3)
            a_(shared_row[:, :], TBK[:, 0:D], ACT.Copy).then_inc(prep_free, 1)
            act.wait_ge(gb_in, 32)
            act.wait_ge(half_up_ready, 1)

            def front_hi(b, par, e, j):
                f, fp = b + 1, 1 - par
                k = (j + fp) % 2
                if j == QUANT:
                    ternary_move((f * FRONT + SHARED_Q + QUANT + 1,),
                                 e, fp == 1, k)
                    return
                act.wait_ge(f_full, f * FRONT + SHARED_Q + j + 1)
                if j in (FC_CTX, FC_X):
                    lo = T if j == FC_CTX else 0
                    a_(xt_hi[:, :, lo:lo + T], fb2[k], ACT.Copy).then_inc(f_hi, 1)
                elif j in (V0, V1, V2, V3):
                    jb = {V0: 0, V1: 1, V2: 2, V3: 3}[j]
                    a_(v_st[fp][:, 0, jb, :, 0:DH], fb_heads[k], ACT.Copy).then_inc(f_hi, 1)
                elif j in (Q0, Q1):
                    at_least(act, q_stacked[j - Q0], f * 64)
                    a_(q_stage[j - Q0][:, :, 0, :], fb2[k], ACT.Copy).then_inc(f_hi, 1)
                else:
                    c = j - K0
                    at_least(act, k_stacked[c % 2], f * 128 + 64 * (c // 2))
                    a_(k_stage[c % 2][:, 0, :], FB[k][:, :], ACT.Copy).then_inc(f_hi, 1)

            def tail_act(b, j):
                t = b - 1
                if j in (OT0, OT1):
                    act.wait_ge(t_full, t * TAIL + j + 1)
                    a_(ot_hi[:, :, :], TBK[:, :].rearrange("p (c t) -> p c t", c=IC), ACT.Copy)\
                        .then_inc(ot_hi_ready, 1)
                elif j == HT:
                    act.wait_ge(t_full, t * TAIL + j + 1)
                    for c in range(DC):
                        last = a_(ht[:, c, :], tb2[:, c, :], ACT.Identity, bias=gb[:, 1, c:c + 1], scale=gb[:, 0, c:c + 1])
                    last.then_inc(ht_ready, 1)
                    act.wait_ge(ht_ready, t + 1)
                    a_(ht_hi[:, :, :], ht[:, :, :], ACT.Copy).then_inc(h_hi_ready, 1)
                elif j == ROUTER:
                    act.wait_ge(t_full, t * TAIL + j + 1)
                    a_(logits[:, bass.ds(t * TB, TB), :], TBK[:, 0:TB * E].rearrange("p (t e) -> p t e", e=E),
                       ACT.Copy).then_inc(logits_ready, 1)
                elif j in (UP0, UP1):
                    act.wait_ge(t_full, t * TAIL + j + 1)
                    for c in range(2):
                        n = 2 * (j - UP0) + c
                        last = a_(th[:, c, :], tb2[:, c, :], ACT.Tanh, scale=half_up[:, n:n + 1])
                    last.then_inc(th_ready, 1)

            def body(b, par, e):
                for u in units_of(b):
                    g = b * UNITS + u
                    if has_front(b) and u - 1 in FRONT_AT:
                        front_hi(b, par, e, FRONT_AT[u - 1])
                    if has_tail(b) and u - 1 in TAIL_AT:
                        tail_act(b, TAIL_AT[u - 1])
                    if (has_attention(b) and not (is_static(b) and b == 0 and u == 0)) or (is_static(b) and b == B and u == 0):
                        act.wait_ge(pt_ready, g)
                        if not (is_static(b) and b == 0 and u < 3):
                            act.wait_ge(pv_done, g - 2)
                        a_(pt_hi[(u + 1) % 2][:, :, :], PT[(u + 1) % 2][:, :].rearrange("p (k i) -> p k i", k=KB),
                           ACT.Copy).then_inc(pt_hi_ready, 1)
                    if has_attention(b):
                        act.wait_ge(max_ready, g + 1)
                        if not (is_static(b) and b == 0 and u < 2):
                            act.wait_ge(pt_ready, g - 1)
                        a_(probs[u % 2][:, :], S[u % 2][:, :], ACT.Exp, bias=neg_max[:, u % 4:u % 4 + 1],
                           accum_out=sums[:, u:u + 1])\
                            .then_inc(probs_ready, 1)

            slots(act, body)

            act.wait_ge(dve_step, 2)
            a_(exps, exps, ACT.Exp, scale=1.0 / RSCALE).then_inc(exps_ready, 1)
            for n in range(4):
                act.wait_ge(rowscale_full, n + 1)
                a_(row_scales[:, 2 * n:2 * n + 2, :], FB[0][:, :].rearrange("p (e d) -> p e d", e=2), ACT.Copy)\
                    .then_inc(rowscale_free, 1)

            def split_ht(a, s):
                act.wait_ge(e_ht_full, a + 1)
                v = S[s][:, 0:DC * P].rearrange("p (c t) -> p c t", c=DC)
                if not (is_static(a) and a < 2):
                    act.wait_ge(e_ht_lo, a - 1)
                for c in range(DC):
                    last = a_(e_htf[s][:, c, :], v[:, c, :], ACT.Identity, bias=gb[:, 1, c:c + 1], scale=gb[:, 0, c:c + 1])
                last.then_inc(e_ht, 1)
                act.wait_ge(e_ht, a + 1)
                if not (is_static(a) and a < 2):
                    act.wait_ge(e_up_full, a - 1)
                a_(e_hth[s], e_htf[s], ACT.Copy).then_inc(e_ht_hi, 1)

            def tanh_and_hi(a, s):
                act.wait_ge(e_u, a + 1)
                a_(e_tanh[s], e_up[s], ACT.Tanh, scale=1.0 / HSCALE).then_inc(e_th, 1)
                act.wait_ge(e_g, a + 1)
                if not (is_static(a) and a < 2):
                    act.wait_ge(e_down_full, a - 1)
                a_(e_gh[s], e_gate[s], ACT.Copy).then_inc(e_g_hi, 1)

            split_ht(0, 0)
            split_ht(1, 1)
            tanh_and_hi(0, 0)
            split_ht(2, 0)
            tanh_and_hi(1, 1)
            with act.Fori(1, SLOTS // 2 - 1) as i:
                split_ht(i * 2 + 1, 1)
                tanh_and_hi(i * 2, 0)
                split_ht(i * 2 + 2, 0)
                tanh_and_hi(i * 2 + 1, 1)
            split_ht(SLOTS - 1, 1)
            tanh_and_hi(SLOTS - 2, 0)
            tanh_and_hi(SLOTS - 1, 1)

        @block.vector
        def _(dve):
            v = nc.vector
            for n in range(5):
                dve.wait_ge(w_hi_ready, n + 1)
                v.scalar_tensor_tensor(w_lo[:, n, :, :].rearrange("p c n -> p (c n)"), landing[n],
                                       QSCALE if n == WQ else 1.0,
                                       w_hi[:, n, :, :].rearrange("p c n -> p (c n)").bitcast(F32),
                                       ALU.mult, ALU.subtract).then_inc(w_lo_ready, 1)
            dve.wait_ge(w_hi_ready, 6)
            v.tensor_tensor(wo_lo[:, :, :], landing[5].rearrange("p (c n) -> p c n", c=IC),
                            wo_hi[:, :, :].bitcast(F32), ALU.subtract).then_inc(w_lo_ready, 1)

            def quantise(n, e, down, stage):
                cols, width = (DC, FW) if down else (FC, D)
                raw = raw_down if down else raw_up
                if stage == 0:
                    row_scale(n, e, cols, width, raw, down)
                    return
                if stage == 1:
                    dve.wait_ge(half_ready, n * 3 + 3)
                    at_least(dve, f_full, quant_job(n - 1))
                if stage < 3:
                    side = w_half[:, stage - 1, 0:cols].unsqueeze(2).broadcast_to([P, cols, 1024 // cols])
                    dst = (above, under)[stage - 1][:, :].rearrange("p (c d) -> p c d", c=cols)
                    v.tensor_tensor(dst, raw, side, ALU.is_gt if stage == 1 else ALU.is_lt).then_inc(sign_ready, 1)
                    return
                dve.wait_ge(sign_ready, n * 2 + 2)
                v.tensor_tensor(above[:, :], above[:, :], under[:, :], ALU.subtract).then_inc(tern_ready, 1)

            def row_scale(n, e, cols, width, raw, down):
                dve.wait_ge(raw_loaded, (n + 1) * 16)
                v.tensor_reduce(w_abs[:, 0:cols], raw, AX.X, ALU.add, apply_absolute_value=True).then_inc(abs_ready, 1)
                dve.wait_ge(abs_ready, n + 1)
                v.tensor_scalar(w_abs[:, 0:cols], w_abs[:, 0:cols], 1.0 / width, EPS, ALU.mult, ALU.max)\
                    .then_inc(scale_ready, 1)
                dve.wait_ge(scale_ready, n + 1)
                v.tensor_scalar(w_half[:, 0, 0:cols], w_abs[:, 0:cols], 0.5, None, ALU.mult).then_inc(half_ready, 1)
                v.tensor_scalar(w_half[:, 1, 0:cols], w_abs[:, 0:cols], -0.5, None, ALU.mult).then_inc(half_ready, 1)
                dst = (down_scale if down else up_scale)[:, bass.ds(e, 1), 0:cols].rearrange("p a c -> p (a c)")
                v.tensor_scalar(dst, w_abs[:, 0:cols], 1.0 / HSCALE if down else HSCALE / 2, None, ALU.mult)\
                    .then_inc(half_ready, 1)
                if is_static(n) and n == 0:
                    v.tensor_scalar(half_up[:, :], w_abs[:, :], 0.5, None, ALU.mult).then_inc(half_up_ready, 1)

            for stage in range(4):
                quantise(0, E, False, stage)
            dve.wait_ge(rw_hi_ready, 1)
            v.scalar_tensor_tensor(rw_lo[:, :, :].rearrange("p c e -> p (c e)"), TBK[:, 0:DC * E], RSCALE,
                                   rw_hi[:, :, :].rearrange("p c e -> p (c e)"), ALU.mult, ALU.subtract)\
                .then_inc(prep_free, 1)
            for stage in range(4):
                quantise(1, E, True, stage)
            dve.wait_ge(half_ready, 6)
            for c in range(DC):
                v.tensor_scalar(diag[:, c, :], ident[:, :], down_scale[:, E, c:c + 1], None, ALU.mult)\
                    .then_inc(diag_ready, 1)

            def settle(s, value):
                dve.wait_ge(s, value)
                v.memset(pause[:, :], 0.0)

            def stats_front(b):
                f = b + 1
                dve.wait_ge(x_loaded, (f + 1) * 16)
                for i in range(TB):
                    v.bn_stats(st1[:, i, :], x_in[:, i, :]).then_inc(stats1, 1)

            def variance_front(b):
                f = b + 1
                settle(stats1, f * 2 + 2)
                for i in range(TB):
                    v.bn_aggr(mv1[:, i, :], st1[:, i, :]).then_inc(var1, 1)
                dve.wait_ge(var1, f * 2 + 2)
                v.tensor_scalar(ve1[:, :], mv1[:, :, 1], EPS, None, ALU.add).then_inc(ve1_ready, 1)

            def normalise_front(b):
                f = b + 1
                dve.wait_ge(rs1_ready, f + 1)
                for i in range(TB):
                    last = v.tensor_scalar(x1[:, i, :], x_in[:, i, :], mv1[:, i, 0:1], rs1[:, i:i + 1],
                                           ALU.subtract, ALU.mult)
                last.then_inc(x1_ready, 1)

            def front_lo(b, par, j):
                f, fp = b + 1, 1 - par
                k = (j + fp) % 2
                if j == QUANT:
                    return
                n = j
                dve.wait_ge(f_hi, f * SPLIT + n + 1)
                if j in (FC_CTX, FC_X):
                    lo = T if j == FC_CTX else 0
                    v.tensor_tensor(xt_lo[:, :, lo:lo + T], fb2[k], xt_hi[:, :, lo:lo + T].bitcast(F32), ALU.subtract)\
                        .then_inc(f_lo, 1)
                elif j in (V0, V1, V2, V3):
                    jb = {V0: 0, V1: 1, V2: 2, V3: 3}[j]
                    v.tensor_tensor(v_st[fp][:, 1, jb, :, 0:DH], fb_heads[k], v_st[fp][:, 0, jb, :, 0:DH], ALU.subtract)\
                        .then_inc(f_lo, 1)
                elif j in (Q0, Q1):
                    s = j - Q0
                    v.tensor_tensor(q_stage[s][:, :, 1, :], fb2[k], q_stage[s][:, :, 0, :], ALU.subtract).then_inc(f_lo, 1)
                else:
                    s = (j - K0) % 2
                    v.tensor_tensor(k_stage[s][:, 1, :], FB[k][:, :], k_stage[s][:, 0, :], ALU.subtract).then_inc(f_lo, 1)

            def normalise_heads(n, k):
                o4 = O[:, (k % 2) * 4 * DH:(k % 2 + 1) * 4 * DH].rearrange("p (h d) -> p h d", h=4)
                dve.wait_ge(pv_done, (n + 1) * 4)
                v.reciprocal(inv_sum[:, :], sums[:, 4 * k:4 * k + 4]).then_inc(inv_ready, 1)
                dve.wait_ge(inv_ready, n + 1)
                dst = o_sb[:, k // 2, (k % 2) * 4 * DH:(k % 2 + 1) * 4 * DH].rearrange("p (h d) -> p h d", h=4)
                v.tensor_tensor(dst, o4[:, :, 0:DH], inv_sum[:, :].unsqueeze(2).broadcast_to([P, 4, DH]), ALU.mult)\
                    .then_inc(normed, 1)

            def tail_dve(b, j):
                t = b - 1
                if j in (OT0, OT1):
                    dve.wait_ge(ot_hi_ready, t * 2 + (j == OT1) + 1)
                    v.tensor_tensor(ot_lo[:, :, :], TBK[:, :].rearrange("p (c t) -> p c t", c=IC),
                                    ot_hi[:, :, :].bitcast(F32), ALU.subtract).then_inc(ot_lo_ready, 1)
                elif j in (WO0, WO1):
                    i = int(j == WO1)
                    dve.wait_ge(t_full, t * TAIL + j + 1)
                    if i == 0:
                        dve.wait_ge(xb_ready, t + 1)
                        at_least(dve, r_ready, t)
                    v.tensor_tensor(x2[:, i, :], TBK[:, 0:D], xb[:, i, :], ALU.add).then_inc(x2_ready, 1)
                elif j in (UP0, UP1):
                    n = j - UP0
                    dve.wait_ge(th_ready, t * 2 + n + 1)
                    v.scalar_tensor_tensor(gate[n][:, :, :].rearrange("p c t -> p (c t)"),
                                           th[:, :, :].rearrange("p c t -> p (c t)"), 1.0, TBK[:, :],
                                           ALU.add, ALU.mult).then_inc(gate_ready, 1)
                elif j == DOWN:
                    dve.wait_ge(t_full, t * TAIL + j + 1)
                    v.tensor_tensor(row[:, :, 0:D], tb2, shared_row[:, :].unsqueeze(1).broadcast_to([P, TB, D]),
                                    ALU.mult).then_inc(shared_ready, 1)

            def residual_stats(b, j):
                t = b - 1
                if j in (WO0, WO1):
                    i = int(j == WO1)
                    dve.wait_ge(x2_ready, t * 2 + i + 1)
                    v.bn_stats(st2[:, i, :], x2[:, i, :]).then_inc(stats2, 1)
                    settle(stats2, t * 2 + i + 1)
                    v.bn_aggr(mv2[:, i, :], st2[:, i, :]).then_inc(var2, 1)
                    if i == TB - 1:
                        dve.wait_ge(var2, t * 2 + 2)
                        v.tensor_scalar(ve2[:, :], mv2[:, :, 1], 1.0 + EPS, EPS * EPS, ALU.mult, ALU.add)\
                            .then_inc(ve2_ready, 1)

            def layernorm_tail(b):
                t = b - 1
                dve.wait_ge(rs2_ready, t + 1)
                at_least(dve, rows_stored, t * 16)
                for i in range(TB):
                    last = v.tensor_scalar(row[:, i, D:2 * D], x2[:, i, :], mv2[:, i, 0:1], rs2[:, i:i + 1],
                                           ALU.subtract, ALU.mult)
                last.then_inc(hn_ready, 1)

            def gate_hi(b, n):
                t = b - 1
                dve.wait_ge(gated, t * 2 + n + 1)
                v.tensor_copy(g_hi[:, 2 * n:2 * n + 2, :], gate[n][:, :, :]).then_inc(g_hi_ready, 1)

            def body(b, par, e):
                for u in units_of(b):
                    g = b * UNITS + u
                    if has_attention(b):
                        dve.wait_ge(scores_ready, g + 1)
                        v.tensor_reduce(neg_max[:, u % 4:u % 4 + 1], S[u % 2][:, :], AX.X, ALU.max, negate=True)\
                            .then_inc(max_ready, 1)
                    if has_front(b) and u - 1 in FRONT_AT:
                        front_lo(b, par, FRONT_AT[u - 1])
                    if has_tail(b) and u - 1 in TAIL_AT:
                        tail_dve(b, TAIL_AT[u - 1])
                    if (has_attention(b) and not (is_static(b) and b == 0 and u == 0)) or (is_static(b) and b == B and u == 0):
                        s = (u + 1) % 2
                        dve.wait_ge(pt_hi_ready, g)
                        v.tensor_tensor(pt_lo[s][:, :, :], PT[s][:, :].rearrange("p (k i) -> p k i", k=KB),
                                        pt_hi[s][:, :, :], ALU.subtract).then_inc(pt_lo_ready, 1)
                    if u % 4 == 1 and ((has_attention(b) and not (is_static(b) and b == 0 and u == 1)) or
                                       (is_static(b) and b == B and u == 1)):
                        normalise_heads(b * 4 + u // 4 - 1, (u // 4 - 1) % 4)
                    if has_front(b):
                        if u == 0:
                            stats_front(b)
                        if u == 1:
                            variance_front(b)
                        if u == 2:
                            normalise_front(b)
                        if u in (4, 6, 8):
                            quantise(b + 1 + SHARED_Q, e, par == 0, u // 2 - 2)
                    if has_tail(b):
                        if u - 1 in TAIL_AT:
                            residual_stats(b, TAIL_AT[u - 1])
                        if u == 7:
                            layernorm_tail(b)
                        if u == 12:
                            gate_hi(b, 0)
                        if u == 13:
                            gate_hi(b, 1)

            slots(dve, body)

            step = [0]

            def then(ins):
                step[0] += 1
                ins.then_inc(dve_step, 1)
                dve.wait_ge(dve_step, step[0])

            def spread(ap, shape, axis):
                return ap.unsqueeze(axis).broadcast_to(shape)

            TE = [P, TILES, E]
            dve.wait_ge(logits_ready, B)
            dve.wait_ge(iota_ready, 7)
            then(v.tensor_reduce(top, logits[:, :, :], AX.X, ALU.max))
            then(v.tensor_tensor(exps, logits[:, :, :], spread(top, TE, 2), ALU.subtract))
            then(v.tensor_tensor(score_e, logits[:, :, :], spread(top, TE, 2), ALU.is_equal))
            then(v.tensor_tensor(score_e, score_e, spread(iota_down, TE, 1), ALU.mult))
            then(v.tensor_reduce(top, score_e, AX.X, ALU.max))
            then(v.tensor_tensor(hot, score_e, spread(top, TE, 2), ALU.is_equal))
            v.tensor_copy(hot16, hot).then_inc(onehot_ready, 1)
            v.tensor_tensor(diag_all.rearrange("p (n k) -> p n k", k=P), spread(ident[:, :], [P, E * DC, P], 1),
                            spread(down_scale[:, 0:E, :].rearrange("p e c -> p (e c)"), [P, E * DC, P], 2),
                            ALU.mult).then_inc(dmat_ready, 1)
            dve.wait_ge(exps_ready, 1)
            then(v.tensor_reduce(esum, exps, AX.X, ALU.add))
            then(v.reciprocal(prob, esum))
            then(v.tensor_copy(p_hi, prob))
            then(v.tensor_tensor(p_lo, prob, p_hi, ALU.subtract))
            dve.wait_ge(ranks_ready, 1)
            then(v.tensor_copy(counts, S[1][:, 0:TILES * E].rearrange("p (t e) -> p t e", e=E)))
            for e in range(E):
                last = v.tensor_tensor_scan(incl[:, :, e], ones32, counts[:, :, e], 0.0, ALU.mult, ALU.add)
            then(last)
            then(v.tensor_copy(total, incl[:, TILES - 1, :]))
            then(v.tensor_tensor(steps32, spread(total, [P, E, TILES], 2), spread(iota_tiles128, [P, E, TILES], 1),
                                 ALU.is_gt))
            then(v.tensor_reduce(tiles_of, steps32, AX.X, ALU.add))
            then(v.tensor_tensor_scan(tile_end, ones32[:, 0:E], tiles_of, 0.0, ALU.mult, ALU.add))
            then(v.tensor_tensor(base, tile_end, tiles_of, ALU.subtract))
            then(v.tensor_scalar(base, base, float(P), None, ALU.mult))
            then(v.tensor_tensor(place, incl, counts, ALU.subtract))
            then(v.tensor_tensor(place, place, S[0][:, 0:TILES * E].rearrange("p (t e) -> p t e", e=E), ALU.add))
            then(v.tensor_tensor(place, place, spread(base, TE, 1), ALU.add))
            then(v.tensor_tensor(place, place, hot, ALU.mult))
            then(v.tensor_reduce(dest, place, AX.X, ALU.add))
            then(v.tensor_copy(desti, dest))
            then(v.tensor_scalar(tilei, desti, 7, None, ALU.arith_shift_right))
            then(v.tensor_scalar(lanei, desti, P - 1, None, ALU.bitwise_and))
            then(v.tensor_copy(slot_tile, tilei))
            then(v.tensor_copy(lane, lanei))
            TL, TA = [P, TILES, P], [P, TILES, SLOTS]
            then(v.tensor_tensor(lane_hot, spread(iota_lane, TL, 1), spread(lane, TL, 2), ALU.is_equal))
            then(v.tensor_tensor(tile_hot, spread(iota_tile, TA, 1), spread(slot_tile, TA, 2), ALU.is_equal))
            v.tensor_tensor(map_ids[:, :, 0, :], tile_hot, spread(iota_tile1, TA, 2), ALU.mult).then_inc(maps_ready, 1)
            v.tensor_scalar(map_ids[:, :, 1, :], tile_hot, iota_p, None, ALU.mult).then_inc(maps_ready, 1)
            v.tensor_tensor(map_probs[:, :, 0, :], tile_hot, spread(p_hi, TA, 2), ALU.mult).then_inc(maps_ready, 1)
            v.tensor_tensor(map_probs[:, :, 1, :], tile_hot, spread(p_lo, TA, 2), ALU.mult).then_inc(maps_ready, 1)
            EA = [P, SLOTS, E]
            owner = gate[0][:, :, :].rearrange("p c t -> p (c t)")[:, 0:SLOTS * E].rearrange("p (a e) -> p a e", e=E)
            then(v.tensor_tensor(owner, spread(tile_end, EA, 1), spread(iota_tile, EA, 2), ALU.is_le))
            then(v.tensor_reduce(tile_e, owner, AX.X, ALU.add))
            then(v.tensor_scalar(tile_e, tile_e, float(E - 1), None, ALU.min))
            then(v.tensor_copy(tile_ei, tile_e))
            dve.wait_ge(slots_ready, 1)
            q_ = TBK[:, 0:2 * SLOTS]
            then(v.tensor_scalar(absent, q_[:, 0:SLOTS], 0.5, float(ABSENT), ALU.is_lt, ALU.mult))
            then(v.scalar_tensor_tensor(slot_id, q_[:, 0:SLOTS], float(P), absent, ALU.mult, ALU.add))
            then(v.tensor_tensor(slot_id, slot_id, q_[:, SLOTS:2 * SLOTS], ALU.add))
            then(v.tensor_scalar(slot_id, slot_id, float(P), None, ALU.subtract))
            then(v.tensor_copy(slot_prob, TBK[:, 2 * SLOTS:3 * SLOTS]))
            then(v.tensor_tensor(slot_prob, slot_prob, TBK[:, 3 * SLOTS:4 * SLOTS], ALU.add))
            v.tensor_copy(slot_idx, slot_id).then_inc(table_ready, 1)

            dve.wait_ge(rowscale_free, 4)
            dve.wait_ge(table_ready, 1)

            def split_lo(a, s):
                dve.wait_ge(e_ht_hi, a + 1)
                v.tensor_tensor(e_htl[s], e_htf[s], e_hth[s], ALU.subtract).then_inc(e_ht_lo, 1)

            def gate_up(a, s):
                e = dve.value_load(tile_ei[0:1, bass.ds(a, 1)], min_val=0, max_val=E - 1)
                dve.wait_ge(e_up_full, a + 1)
                sc = up_scale[:, bass.ds(e, 1), :].rearrange("p a c -> p (a c)")
                v.tensor_tensor(e_up[s].rearrange("p (c t) -> p c t", c=FC),
                                PT[s][:, :].rearrange("p (c t) -> p c t", c=FC),
                                spread(sc, [P, FC, P], 2), ALU.mult).then_inc(e_u, 1)
                return e

            def gate_out(a, s):
                dve.wait_ge(e_th, a + 1)
                v.scalar_tensor_tensor(e_gate[s], e_tanh[s], 1.0, e_up[s], ALU.add, ALU.mult).then_inc(e_g, 1)
                dve.wait_ge(e_g_hi, a + 1)
                v.tensor_tensor(e_gl[s], e_gate[s], e_gh[s], ALU.subtract).then_inc(e_g_lo, 1)

            def scale_out(a, s):
                e = dve.value_load(tile_ei[0:1, bass.ds(a, 1)], min_val=0, max_val=E - 1)
                dve.wait_ge(e_down_full, a + 1)
                if not (is_static(a) and a < 2):
                    dve.wait_ge(e_out, a - 1)
                v.scalar_tensor_tensor(e_yv[s], OE[s], slot_prob[:, bass.ds(a, 1)],
                                       row_scales[:, bass.ds(e, 1), :].rearrange("p a d -> p (a d)"),
                                       ALU.mult, ALU.mult).then_inc(e_y, 1)

            def round_(a):
                split_lo(a, 1)
                gate_up(a - 1, 0)
                gate_out(a - 1, 0)
                if not (is_static(a) and a < 2):
                    scale_out(a - 2, 1)
                split_lo(a + 1, 0)
                gate_up(a, 1)
                gate_out(a, 1)
                scale_out(a - 1, 0)

            split_lo(0, 0)
            round_(1)
            round_(3)
            with dve.Fori(2, SLOTS // 2 - 1) as i:
                round_(i * 2 + 1)
            split_lo(SLOTS - 1, 1)
            gate_up(SLOTS - 2, 0)
            gate_out(SLOTS - 2, 0)
            scale_out(SLOTS - 3, 1)
            gate_up(SLOTS - 1, 1)
            gate_out(SLOTS - 1, 1)
            scale_out(SLOTS - 2, 0)
            scale_out(SLOTS - 1, 1)

        @block.tensor
        def _(pe):
            mm = nc.tensor.matmul
            pe.wait_ge(const_ready, 9)

            def transpose_ternary(n, down, k):
                pe.wait_ge(tern_ready, n + 1)
                for i in range(8):
                    outer, inner = (i // DC, i % DC) if down else (i // FC, i % FC)
                    cols, width = (inner * FW + outer * P, FW) if down else (inner * D + outer * P, D)
                    last = nc.tensor.transpose(fb16[k][:, i * P:(i + 1) * P], above[:, cols:cols + P], ident16[:, :])
                last.then_inc(f_full, 1)

            transpose_ternary(0, False, 1)
            pe.wait_ge(rw_in, 16)
            for c in range(DC):
                last = nc.tensor.transpose(TBK[:, c * E:(c + 1) * E], small[0:E, c * P:(c + 1) * P], ident[0:E, 0:E])
            last.then_inc(prep_full, 1)
            pe.wait_ge(tern_moved, 1)
            transpose_ternary(1, True, 1)
            pe.wait_ge(small_in, 16)
            pe.wait_ge(prep_free, 1)
            mm(TBK[:, 0:D], ones[0:1, :], small[0:1, :], start=True, stop=True).then_inc(prep_full, 1)
            pe.wait_ge(diag_ready, DC)
            pe.wait_ge(prep_free, 2)
            mm(TBK[:, 0:D], ones[:, :], diag[:, :, :], start=True, stop=True).then_inc(prep_full, 1)
            pe.wait_ge(prep_free, PREP)
            pe.wait_ge(w_lo_ready, 6)

            def front_job(b, par, j):
                f, fp = b + 1, 1 - par
                k = (j + fp) % 2
                if j == FC_CTX:
                    at_least(pe, f_lo, f * SPLIT)
                    pe.wait_ge(c_loaded, (f + 1) * 16)
                elif j in (V2, Q0):
                    pe.wait_ge(f_lo, f * SPLIT + j)
                else:
                    pe.wait_ge(f_lo, f * SPLIT + j - 1)
                if j == V2:
                    pe.wait_ge(tern_moved, f + SHARED_Q)
                if j in (FC_CTX, FC_X):
                    if j == FC_X:
                        pe.wait_ge(x1_ready, f + 1)
                    src = c_in if j == FC_CTX else x1
                    for i in range(TB):
                        for c in range(DC):
                            last = nc.tensor.transpose(fb2[k][:, c, i * P:(i + 1) * P], src[:, i, c * P:(c + 1) * P],
                                                       ident[:, :])
                elif j in (V0, V1, V2, V3):
                    jb = {V0: 0, V1: 1, V2: 2, V3: 3}[j]
                    w = WV1 if jb < TB else WV2
                    cols = slice(jb * P, (jb + 1) * P)
                    last = split_product(FB[k][:, :], [(xt_hi[:, c, cols], xt_lo[:, c, cols], w_hi[:, w, c, :], w_lo[:, w, c, :])
                                                    for c in range(DC)])
                elif j in (Q0, Q1):
                    for n in range(2):
                        cols = slice((2 * (j - Q0) + n) * P, (2 * (j - Q0) + n + 1) * P)
                        last = split_product(fb2[k][:, n, :], [(w_hi[:, WQ, c, cols], w_lo[:, WQ, c, cols],
                                                             xt_hi[:, c, 0:T], xt_lo[:, c, 0:T]) for c in range(DC)])
                elif j == QUANT:
                    transpose_ternary(f + SHARED_Q, fp == 1, k)
                    return
                else:
                    cols = slice((j - K0) * P, (j - K0 + 1) * P)
                    for n, w in enumerate((WK1, WK2)):
                        last = split_product(fb2[k][:, n, :], [(w_hi[:, w, c, cols], w_lo[:, w, c, cols],
                                                                xt_hi[:, c, n * T:(n + 1) * T], xt_lo[:, c, n * T:(n + 1) * T])
                                                            for c in range(DC)])
                last.then_inc(f_full, 1)

            def scores(b, par, u):
                g = b * UNITS + u
                ib, h = u // HEADS, u % HEADS
                if u == 0:
                    for s in range(2):
                        pe.wait_ge(q_stacked[s], (b + 1) * 64)
                        pe.wait_ge(k_stacked[s], (b + 1) * 128)
                if not (is_static(b) and b == 0 and u < 2):
                    pe.wait_ge(probs_ready, g - 1)
                for k in range(2):
                    last = mm(S[u % 2][:, :], q_st[par][:, h, k, ib * P:(ib + 1) * P], k_st[par][:, h, :],
                              start=(k == 0), stop=(k == 1))
                last.then_inc(scores_ready, 1)

            def transpose_probs(g, s, ring):
                pe.wait_ge(probs_ready, g + 1)
                if ring:
                    pe.wait_ge(pt_lo_ready, g - 1)
                for k in range(KB):
                    last = nc.tensor.transpose(PT[s][:, k * P:(k + 1) * P], probs[s][:, k * P:(k + 1) * P], ident[:, :])
                last.then_inc(pt_ready, 1)

            def weigh_values(g, u, par, group, ring):
                h = u % HEADS
                if u % 4 == 0 and ring:
                    pe.wait_ge(normed, group)
                pe.wait_ge(pt_lo_ready, g + 1)
                o1 = O[:, h * DH:(h + 1) * DH]
                for jb in range(KB):
                    mm(o1, pt_hi[u % 2][:, jb, :], v_st[par][:, 0, jb, h, :], start=(jb == 0), stop=False)
                    mm(o1, pt_hi[u % 2][:, jb, :], v_st[par][:, 1, jb, h, :], start=False, stop=False)
                    last = mm(o1, pt_lo[u % 2][:, jb, :], v_st[par][:, 0, jb, h, :], start=False, stop=(jb == KB - 1))
                last.then_inc(pv_done, 1)

            def tail_job(b, j):
                t = b - 1
                read, count = {OT0: (shared_ready, t), WO0: (ot_lo_ready, t * 2 + 1), OT1: (x2_ready, t * 2 + 1),
                               WO1: (ot_lo_ready, t * 2 + 2), HT: (x2_ready, t * 2 + 2), ROUTER: (ht_ready, t + 1),
                               UP0: (logits_ready, t + 1), UP1: (gate_ready, t * 2 + 1),
                               DOWN: (gate_ready, t * 2 + 2)}[j]
                at_least(pe, read, count)
                if j in (OT0, OT1):
                    i = int(j == OT1)
                    pe.wait_ge(normed, t * 4 + 2 * i + 2)
                    for c in range(IC):
                        last = nc.tensor.transpose(TBK[:, c * P:(c + 1) * P], o_sb[:, i, c * P:(c + 1) * P], ident[:, :])
                elif j in (WO0, WO1):
                    last = split_product(TBK[:, 0:D], [(ot_hi[:, c, :], ot_lo[:, c, :], wo_hi[:, c, :], wo_lo[:, c, :])
                                                       for c in range(IC)])
                elif j == HT:
                    pe.wait_ge(hn_ready, t + 1)
                    for i in range(TB):
                        for c in range(DC):
                            last = nc.tensor.transpose(tb2[:, c, i * P:(i + 1) * P], row[:, i, D + c * P:D + (c + 1) * P],
                                                       ident[:, :])
                elif j == ROUTER:
                    pe.wait_ge(h_lo_ready, t + 1)
                    for i in range(TB):
                        tok = slice(i * P, (i + 1) * P)
                        last = split_product(TBK[:, i * E:(i + 1) * E],
                                             [(ht_hi[:, c, tok], ht_lo[:, c, tok], rw_hi[:, c, :], rw_lo[:, c, :])
                                              for c in range(DC)])
                elif j in (UP0, UP1):
                    for k in range(2):
                        n = 2 * (j - UP0) + k
                        for c in range(DC):
                            w = up16[:, E, c, n * P:(n + 1) * P]
                            mm(tb2[:, k, :], w, ht_hi[:, c, :], start=(c == 0), stop=False)
                            last = mm(tb2[:, k, :], w, ht_lo[:, c, :], start=False, stop=(c == DC - 1))
                else:
                    pe.wait_ge(g_lo_ready, t * 2 + 2)
                    for i in range(TB):
                        tok = slice(i * P, (i + 1) * P)
                        for c in range(FC):
                            mm(tb2[:, i, :], g_hi[:, c, tok], down16[:, E, c, :], start=(c == 0), stop=False)
                            last = mm(tb2[:, i, :], g_lo[:, c, tok], down16[:, E, c, :], start=False, stop=(c == FC - 1))
                last.then_inc(t_full, 1)

            def values(b, par, u):
                last = is_static(b) and b == B
                if (has_attention(b) and not (is_static(b) and b == 0 and u < 2)) or (last and u < 2):
                    g, pu = b * UNITS + u, (u - 2) % UNITS
                    pp = par if u >= 2 else 1 - par
                    weigh_values(g - 2, pu, pp, b * 4 + (u - 2) // 4, not (is_static(b) and g - 2 < 4))

            def body(b, par, e):
                last_slot = is_static(b) and b == B
                for u in units_of(b):
                    g = b * UNITS + u
                    if (has_attention(b) and not (is_static(b) and b == 0 and u == 0)) or (last_slot and u == 0):
                        transpose_probs(g - 1, (u + 1) % 2, not (is_static(b) and g - 1 < 2))
                    late = u % 4 == 2
                    if not late:
                        values(b, par, u)
                    if u + 1 < UNITS and has_attention(b):
                        scores(b, par, u + 1)
                    elif u + 1 == UNITS and (not is_static(b) or b + 1 < B):
                        scores(b + 1, 1 - par, 0)
                    if has_tail(b) and u in TAIL_AT:
                        tail_job(b, TAIL_AT[u])
                    if has_front(b) and u in FRONT_AT:
                        front_job(b, par, FRONT_AT[u])
                    if late:
                        values(b, par, u)

            slots(pe, body)

            pe.wait_ge(onehot_ready, 1)
            mm(S[0][:, 0:TILES * E], below16[:, :], hot16, start=True, stop=True)
            mm(S[1][:, 0:TILES * E], ones16[:, :], hot16, start=True, stop=True).then_inc(ranks_ready, 1)
            pe.wait_ge(dmat_ready, 1)
            for n in range(4):
                at_least(pe, rowscale_free, n)
                mm(FB[0][:, :], ones[:, :], diag_all[:, n * 512:(n + 1) * 512], start=True, stop=True)\
                    .then_inc(rowscale_full, 1)
            pe.wait_ge(maps_ready, 4)
            for n, m in enumerate((map_ids, map_probs)):
                for i in range(TILES):
                    last = mm(TBK[:, n * 2 * SLOTS:(n + 1) * 2 * SLOTS].rearrange("p (g a) -> p g a", g=2),
                              lane_hot[:, i, :], m[:, i, :, :], start=(i == 0), stop=(i == TILES - 1))
            last.then_inc(slots_ready, 1)
            pe.wait_ge(table_ready, 1)

            def rows_to_columns(a, s, k, n):
                pe.wait_ge(gathered[k], (n + 1) * 16)
                if not (is_static(a) and a < 2):
                    pe.wait_ge(e_ht, a - 1)
                for c in range(DC):
                    last = nc.tensor.transpose(S[s][:, c * P:(c + 1) * P], g_rows[k][:, D + c * P:D + (c + 1) * P],
                                               ident[:, :])
                last.then_inc(e_ht_full, 1)

            def up(a, s):
                e = pe.value_load(tile_ei[0:1, bass.ds(a, 1)], min_val=0, max_val=E - 1)
                pe.wait_ge(e_ht_lo, a + 1)
                if not (is_static(a) and a < 2):
                    pe.wait_ge(e_u, a - 1)
                for n in range(FC):
                    for c in range(DC):
                        w = up16[:, bass.ds(e, 1), c, n * P:(n + 1) * P].rearrange("p a f -> p (a f)")
                        o1 = PT[s][:, n * P:(n + 1) * P]
                        mm(o1, w, e_hth[s][:, c, :], start=(c == 0), stop=False)
                        last = mm(o1, w, e_htl[s][:, c, :], start=False, stop=(c == DC - 1))
                last.then_inc(e_up_full, 1)

            def down(a, s):
                e = pe.value_load(tile_ei[0:1, bass.ds(a, 1)], min_val=0, max_val=E - 1)
                pe.wait_ge(e_g_lo, a + 1)
                if not (is_static(a) and a < 2):
                    pe.wait_ge(e_y, a - 1)
                for c in range(FC):
                    w = down16[:, bass.ds(e, 1), c, :].rearrange("p a d -> p (a d)")
                    mm(OE[s], e_gh[s][:, c * P:(c + 1) * P], w, start=(c == 0), stop=False)
                    last = mm(OE[s], e_gl[s][:, c * P:(c + 1) * P], w, start=False, stop=(c == FC - 1))
                last.then_inc(e_down_full, 1)

            def round_(a, k, n):
                up(a - 1, 1)
                down(a - 2, 0)
                rows_to_columns(a, 0, k, n)
                up(a, 0)
                down(a - 1, 1)
                rows_to_columns(a + 1, 1, k + 1, n)

            rows_to_columns(0, 0, 0, 0)
            rows_to_columns(1, 1, 1, 0)
            up(0, 0)
            round_(2, 2, 0)
            with pe.Fori(1, SLOTS // RING) as i:
                round_(i * RING, 0, i)
                round_(i * RING + 2, 2, i)
            up(SLOTS - 1, 1)
            down(SLOTS - 2, 0)
            down(SLOTS - 1, 1)


_INS = ["x", "ctx_1024", "L0_xattn_Wq1", "L0_xattn_Wk1", "L0_xattn_Wv1", "L0_xattn_Wk2", "L0_xattn_Wv2",
        "L0_xattn_Wo", "L0_xattn_bo", "L0_ffn_shared_w1", "L0_ffn_shared_w2", "L0_ffn_expert_w1",
        "L0_ffn_expert_w2", "L0_ffn_router_w", "L0_ffn_ln_gamma", "L0_ffn_ln_beta"]


def kernel(**inputs):
    import numpy as np
    import concourse.bacc as bacc
    from concourse.bass_utils import run_bass_kernel_spmd

    nc = bacc.Bacc("TRN2", target_bir_lowering=False, num_devices=1)
    arrays, args = {}, []
    for name in _INS:
        a = np.ascontiguousarray(inputs[name])
        arrays[f"in_{name}"] = a
        args.append(nc.dram_tensor(f"in_{name}", a.shape, mybir.dt.from_np(a.dtype), kind="ExternalInput").ap())
    out = nc.dram_tensor("out", [B * T, D], F32, kind="ExternalOutput").ap()
    xattn_ffn(nc, *args, out)
    r = run_bass_kernel_spmd(nc, [arrays], core_ids=[0])
    return r.results[0]["out"].reshape(B, T, D)
```

```python
from contextlib import ExitStack

import concourse.bass as bass
from concourse import mybir

F32 = mybir.dt.float32
F16 = mybir.dt.float16
F32R = mybir.dt.float32r
I32 = mybir.dt.int32
U32 = mybir.dt.uint32
ALU = mybir.AluOpType
ACT = mybir.ActivationFunctionType
AX = mybir.AxisListType

P = 128
B, T, D = 16, 256, 256
HEADS, DH = 8, 64
INNER = HEADS * DH
KEYS = 2 * T
DC = D // P
IC = INNER // P
TB = T // P
KB = KEYS // P
UNITS = TB * HEADS
E, FW = 8, 512
FC = FW // P
EPS = 1e-5
QSCALE = DH ** -0.5
HSCALE = 16.0
RSCALE = 64.0
TILES = B * TB
SLOTS = TILES + E
RING = 8
ABSENT = 8192

FC_CTX, V2, FC_X, V3, Q0, Q1, K0, K1, K2, K3, V0, QUANT, V1 = range(13)
FRONT_AT = {0: FC_CTX, 2: V2, 3: FC_X, 5: V3, 6: Q0, 8: Q1, 9: K0, 10: K1, 11: K2, 12: K3, 13: V0, 14: QUANT, 15: V1}
FRONT = 13
SPLIT = 12
OT0, WO0, OT1, WO1, HT, UP0, UP1, DOWN = range(8)
TAIL_AT = {3: OT0, 4: WO0, 6: OT1, 7: WO1, 10: HT, 13: UP0, 14: UP1}
DOWN_AT = 2
TAIL = 8
HT_AT = next(u for u in TAIL_AT if TAIL_AT[u] == HT)
SUMS_AT = 1
NORM_X_AT = 2
NORM_H_AT = 9
GATE_HI_AT = {14: 0}
QUANTISE_AT = {4: 0, 7: 1, 10: 2}
SHARED_Q = 2
ROUTER_W, BIAS, SHARED_UP, SHARED_DOWN, SHARED_ROW = range(5)
PREP_AT = {-1: {6: ROUTER_W, 7: BIAS, 8: SHARED_UP}, 0: {4: SHARED_DOWN, 6: SHARED_ROW}}
PREP = 5


def xattn_ffn(nc, x, ctx_in, wq1, wk1, wv1, wk2, wv2, wo, bo, sw1, sw2, ew1, ew2, router_w, gamma, beta, out):
    rows = nc.dram_tensor("rows", [B * T, 2 * D], F32, kind="Internal").ap()
    with ExitStack() as ctx:
        def sb(name, shape, dt):
            return ctx.enter_context(nc.sbuf_tensor(name, shape, dt))

        def bank(name):
            return ctx.enter_context(nc.psum_tensor(name, [P, 512], F32))

        def sem(name):
            return ctx.enter_context(nc.semaphore(name))

        ident = sb("ident", [P, P], F32)
        ident16 = sb("ident16", [P, P], F16)
        ones = sb("ones", [P, P], F32)
        below16 = sb("below16", [P, P], F16)
        ones16 = sb("ones16", [P, P], F16)
        minus_half = sb("minus_half", [P, TB], F32)
        WV2, WQ, WK1, WK2, WV1 = range(5)
        w_hi = sb("w_hi", [P, 5, DC, INNER], F32R)
        w_lo = sb("w_lo", [P, 5, DC, INNER], F32R)
        wo_hi = sb("wo_hi", [P, IC, D], F32R)
        wo_lo = sb("wo_lo", [P, IC, D], F32R)
        up16 = sb("up16", [P, E + 1, DC, FW], F16)
        down16 = sb("down16", [P, E + 1, FC, D], F16)
        up_scale = sb("up_scale", [P, E + 1, FC], F32)
        down_scale = sb("down_scale", [P, E + 1, DC], F32)
        half_up = sb("half_up", [P, FC], F32)
        shared_row = sb("shared_row", [P, D], F32)
        gb = sb("gb", [P, 2, DC], F32)
        bo_row = sb("bo_row", [P, D], F32)
        rw_hi = sb("rw_hi", [P, DC, E], F16)
        rw_lo = sb("rw_lo", [P, DC, E], F16)
        x_in = sb("x_in", [P, TB, D], F32)
        c_in = sb("c_in", [P, TB, D], F32)
        x1 = sb("x1", [P, TB, D], F32)
        st1 = sb("st1", [P, TB, 6], F32)
        mv1 = sb("mv1", [P, TB, 2], F32)
        ve1 = sb("ve1", [P, TB], F32)
        rs1 = sb("rs1", [P, TB], F32)
        neg_mean1 = sb("neg_mean1", [P, TB], F32)
        shift1 = sb("shift1", [P, TB], F32)
        xt_hi = sb("xt_hi", [P, DC, KEYS], F32R)
        xt_lo = sb("xt_lo", [P, DC, KEYS], F32R)
        q_stage = [sb(f"q_stage{i}", [P, 2, 2, T], F16) for i in range(2)]
        k_stage = [sb(f"k_stage{i}", [P, 2, KEYS], F16) for i in range(3)]
        q_st = [sb(f"q_st{i}", [P, HEADS, 2, T], F16) for i in range(2)]
        k_st = [sb(f"k_st{i}", [P, HEADS, KEYS], F16) for i in range(2)]
        v_st = [sb(f"v_st{i}", [P, 2, KB, HEADS, DH], F16) for i in range(2)]
        pause = sb("pause", [P, 1], F32)
        w_raw = sb("w_raw", [P, 1024], F32)
        w_abs = sb("w_abs", [P, FC], F32)
        w_half = sb("w_half", [P, 2, FC], F32)
        above = sb("above", [P, 1024], F16)
        under = sb("under", [P, 1024], F16)
        probs = [sb(f"probs{i}", [P, KEYS], F32) for i in range(2)]
        neg_max = sb("neg_max", [P, 4], F32)
        pt_hi = [sb(f"pt_hi{i}", [P, KB, P], F16) for i in range(2)]
        pt_lo = [sb(f"pt_lo{i}", [P, KB, P], F16) for i in range(2)]
        sums = sb("sums", [P, UNITS], F32)
        inv_sum = sb("inv_sum", [P, 4], F32)
        o_sb = sb("o_sb", [P, TB, INNER], F32)
        ot_hi = sb("ot_hi", [P, IC, P], F32R)
        ot_lo = sb("ot_lo", [P, IC, P], F32R)
        xb = sb("xb", [P, TB, D], F32)
        x2 = sb("x2", [P, TB, D], F32)
        st2 = sb("st2", [P, TB, 6], F32)
        mv2 = sb("mv2", [P, TB, 2], F32)
        ve2 = sb("ve2", [P, TB], F32)
        rs2 = sb("rs2", [P, TB], F32)
        neg_mean2 = sb("neg_mean2", [P, TB], F32)
        shift2 = sb("shift2", [P, TB], F32)
        row = sb("row", [P, TB, 2 * D], F32)
        ht = sb("ht", [P, DC, T], F32)
        ht_hi = sb("ht_hi", [P, DC, T], F16)
        ht_lo = sb("ht_lo", [P, DC, T], F16)
        logits = sb("logits", [P, TILES, E], F32)
        th = sb("th", [P, 2, T], F32)
        gate = [sb(f"gate{i}", [P, 2, T], F32) for i in range(2)]
        g_hi = sb("g_hi", [P, FC, T], F16)
        g_lo = sb("g_lo", [P, FC, T], F16)
        rw_raw = gate[0][0:E, 0, :]
        bo_raw = gate[1][0:1, 0, :]

        S = [bank("S0"), bank("S1")]
        PT = [bank("PT0"), bank("PT1")]
        O = bank("O")
        FB = [bank("FB0"), bank("FB1")]
        TBK = bank("TBK")

        const_ready = sem("const_ready")
        weights_in = [sem(f"weights_in{i}") for i in range(6)]
        bo_in = sem("bo_in")
        rw_in = sem("rw_in")
        gb_in = sem("gb_in")
        w_hi_ready = sem("w_hi_ready")
        w_lo_ready = sem("w_lo_ready")
        prep_full = sem("prep_full")
        prep_free = sem("prep_free")
        rw_hi_ready = sem("rw_hi_ready")
        diag_ready = sem("diag_ready")
        x_loaded = sem("x_loaded")
        c_loaded = sem("c_loaded")
        stats1 = sem("stats1")
        var1 = sem("var1")
        ve1_ready = sem("ve1_ready")
        rs1_ready = sem("rs1_ready")
        shift1_ready = sem("shift1_ready")
        x1_ready = sem("x1_ready")
        f_full = sem("f_full")
        f_hi = sem("f_hi")
        f_lo = sem("f_lo")
        q_stacked = [sem("q_stacked0"), sem("q_stacked1")]
        k_stacked = [sem(f"k_stacked{i}") for i in range(IC)]
        raw_loaded = sem("raw_loaded")
        raw_by_pool = sem("raw_by_pool")
        abs_ready = sem("abs_ready")
        scale_ready = sem("scale_ready")
        half_ready = sem("half_ready")
        half_up_ready = sem("half_up_ready")
        sign_ready = sem("sign_ready")
        tern_ready = sem("tern_ready")
        tern_moved = sem("tern_moved")
        scores_ready = sem("scores_ready")
        max_ready = sem("max_ready")
        probs_ready = sem("probs_ready")
        pt_ready = sem("pt_ready")
        pt_hi_ready = sem("pt_hi_ready")
        pt_lo_ready = sem("pt_lo_ready")
        pv_done = sem("pv_done")
        inv_ready = sem("inv_ready")
        normed = sem("normed")
        t_full = sem("t_full")
        route_full = sem("route_full")
        ot_lo_ready = sem("ot_lo_ready")
        ht_ready = sem("ht_ready")
        logits_ready = sem("logits_ready")
        ot_hi_ready = sem("ot_hi_ready")
        xr_loaded = sem("xr_loaded")
        xb_ready = sem("xb_ready")
        x2_ready = sem("x2_ready")
        stats2 = sem("stats2")
        var2 = sem("var2")
        ve2_ready = sem("ve2_ready")
        rs2_ready = sem("rs2_ready")
        shift2_ready = sem("shift2_ready")
        hn_ready = sem("hn_ready")
        h_hi_ready = sem("h_hi_ready")
        h_lo_ready = sem("h_lo_ready")
        th_ready = sem("th_ready")
        gate_ready = sem("gate_ready")
        gated = sem("gated")
        g_hi_ready = sem("g_hi_ready")
        g_lo_ready = sem("g_lo_ready")
        shared_ready = sem("shared_ready")
        r_ready = sem("r_ready")
        rows_stored = sem("rows_stored")
        iota_ready = sem("iota_ready")
        dve_step = sem("dve_step")
        exps_ready = sem("exps_ready")
        onehot_ready = sem("onehot_ready")
        ranks_ready = sem("ranks_ready")
        maps_ready = sem("maps_ready")
        slots_ready = sem("slots_ready")
        table_ready = sem("table_ready")
        dmat_ready = sem("dmat_ready")
        rowscale_full = sem("rowscale_full")
        rowscale_free = sem("rowscale_free")
        zeroed = sem("zeroed")
        gathered = [sem(f"gathered{i}") for i in range(RING)]
        e_ht_full = sem("e_ht_full")
        e_ht = sem("e_ht")
        e_ht_hi = sem("e_ht_hi")
        e_ht_lo = sem("e_ht_lo")
        e_up_full = sem("e_up_full")
        e_u = sem("e_u")
        e_th = sem("e_th")
        e_g = sem("e_g")
        e_g_hi = sem("e_g_hi")
        e_g_lo = sem("e_g_lo")
        e_down_full = sem("e_down_full")
        e_y = sem("e_y")
        e_out = sem("e_out")
        stored = [sem("stored0"), sem("stored1")]

        block = ctx.enter_context(nc.Block())

        def at_least(eng, s, value):
            if isinstance(value, int) and value <= 0:
                return
            eng.wait_ge(s, value)

        def slots(eng, body):
            for b in range(-1, 2):
                body(b, b % 2, (b + 1) // 2)
            with eng.Fori(1, B // 2 - 1) as i:
                body(i * 2, 0, i)
                body(i * 2 + 1, 1, i + 1)
            for b in range(B - 2, B + 2):
                body(b, b % 2, (b + 1) // 2)

        def tiles(eng, step):
            def lookup(held):
                def expert(k, c, back):
                    if c - back not in held:
                        held[c - back] = eng.value_load(tile_ei[0:1, bass.ds(k - back, 1)], min_val=0, max_val=E - 1)
                    return held[c - back]
                return expert

            first = lookup({})
            for k in range(-2, 5):
                step(k, k % RING, k // RING, lambda back, k=k: first(k, k, back))
            with eng.Fori(0, (SLOTS - RING) // RING) as i:
                loop = lookup({})
                for k in range(5, 5 + RING):
                    step(i * RING + k, k % RING, i + k // RING, lambda back, k=k: loop(i * RING + k, k, back))
            final = lookup({})
            for k in range(SLOTS - RING + 5, SLOTS + 3):
                step(k, k % RING, k // RING, lambda back, k=k: final(k, k, back))

        def tile_in_range(a):
            return not isinstance(a, int) or 0 <= a < SLOTS

        def is_static(b):
            return isinstance(b, int)

        def has_front(b):
            return not is_static(b) or b + 1 < B

        def has_attention(b):
            return not is_static(b) or 0 <= b < B

        def has_tail(b):
            return not is_static(b) or 1 <= b <= B

        def has_down(b):
            return not is_static(b) or b >= 2

        def units_of(b):
            return range(UNITS)

        def matrix_of(f):
            return 1 if is_static(f) and f == 0 else f + 2

        def split_product(o, pairs):
            terms = [t for (lh, ll, rh, rl) in pairs for t in ((lh, rh), (lh, rl), (ll, rh))]
            for n, (l, r) in enumerate(terms):
                mm = nc.tensor.matmul(o, l, r, start=(n == 0), stop=(n == len(terms) - 1))
            return mm

        x_v = x.rearrange("b (t p) d -> b p t d", p=P)
        c_v = ctx_in.rearrange("b (t p) d -> b p t d", p=P)
        rows_v = rows.rearrange("(b t p) d -> b p t d", p=P, t=TB)
        ew1_v = ew1.rearrange("e (c p) d -> e p c d", p=P)
        ew2_v = ew2.rearrange("e (c p) f -> e p c f", p=P)
        raw_up = w_raw[:, :].rearrange("p (c d) -> p c d", c=FC)
        raw_down = w_raw[:, :].rearrange("p (c f) -> p c f", c=DC)
        fb2 = [a[:, :].rearrange("p (c t) -> p c t", c=2) for a in FB]
        fb_heads = [a[:, :].rearrange("p (h d) -> p h d", h=HEADS) for a in FB]
        fb16 = [a[:, :].bitcast(F16) for a in FB]
        tb16 = TBK[:, :].bitcast(F16)
        tb2 = TBK[:, :].rearrange("p (c t) -> p c t", c=2)
        landing = [k_st[0][:, 0:4, :], k_st[0][:, 4:8, :], k_st[1][:, 0:4, :], k_st[1][:, 4:8, :],
                   q_st[1][:, 0:4, :, :].rearrange("p h a t -> p h (a t)"), q_st[1][:, 4:8, :, :].rearrange("p h a t -> p h (a t)")]
        landing = [a.rearrange("p a b -> p (a b)").bitcast(F32) for a in landing]
        diag = row[:, 0, 0:2 * P].rearrange("p (c t) -> p c t", c=DC)

        def as_floats(ap, form):
            return ap.rearrange(form).bitcast(F32)

        map_columns = TILES * 2 * SLOTS
        spare = [as_floats(v_st[1][:, :, :, :, :], "p a b h t -> p (a b h t)"),
                 as_floats(v_st[0][:, :, :, :, :], "p a b h t -> p (a b h t)")[:, map_columns // 2:],
                 above[:, :].bitcast(F32), under[:, :].bitcast(F32)]
        spare += [as_floats(a[:, :, :, :], "p c k t -> p (c k t)") for a in q_stage]
        spare = [[a, a.shape[1]] for a in spare]

        def piece(n):
            room = next(a for a in spare if a[1] >= n)
            room[1] -= n
            return room[0][:, room[1]:room[1] + n]

        scale_terms = piece(SLOTS * FC * E).rearrange("p (c a e) -> p c a e", a=SLOTS, c=FC)
        score_e, hot, exps, incl, counts, place = (piece(TILES * E).rearrange("p (t e) -> p t e", e=E) for _ in range(6))
        steps32 = piece(E * TILES).rearrange("p (e t) -> p e t", e=E)
        owner = piece(SLOTS * E).rearrange("p (a e) -> p a e", e=E)
        tile_scale = piece(SLOTS * FC).rearrange("p (a c) -> p a c", a=SLOTS)
        hot16 = piece(TILES * E // 2).bitcast(F16).rearrange("p (t e) -> p t e", e=E)
        top, dest, slot_tile, lane, prob, esum = (piece(TILES) for _ in range(6))
        total, tiles_of, tile_end, base = (piece(E) for _ in range(4))
        desti, tilei, lanei = (piece(TILES).bitcast(I32) for _ in range(3))
        slot_prob, slot_id, tile_e, absent = (piece(SLOTS) for _ in range(4))
        slot_idx = piece(SLOTS).bitcast(U32)
        tile_ei = piece(SLOTS).bitcast(I32)
        p_hi, p_lo = (piece(TILES // 2).bitcast(F16) for _ in range(2))
        iota_lane = x_in[:, 0, 0:P]
        iota_tile = x_in[:, 0, P:P + SLOTS]
        iota_tiles128 = x_in[:, 1, 0:TILES]
        iota_tile1 = x_in[:, 1, 32:32 + TILES]
        iota_down = x_in[:, 1, 64:64 + E]
        iota_p = x_in[:, 1, 96:97]
        ones32 = x_in[:, 1, 128:128 + TILES]
        lane_hot = q_st[0][:, :, :, :].rearrange("p a h t -> p (a h t)").rearrange("p (t l) -> p t l", l=P)
        tile_hot = w_raw[:, :].bitcast(F16)[:, 0:TILES * SLOTS].rearrange("p (t a) -> p t a", a=SLOTS)
        map_ids = q_st[1][:, :, :, :].rearrange("p a h t -> p (a h t)")[:, 0:TILES * 2 * SLOTS]\
            .rearrange("p (t g a) -> p t g a", g=2, a=SLOTS)
        map_probs = v_st[0][:, :, :, :, :].rearrange("p a b h t -> p (a b h t)")[:, 0:TILES * 2 * SLOTS]\
            .rearrange("p (t g a) -> p t g a", g=2, a=SLOTS)
        diag_all = k_st[1][:, :, :].rearrange("p a b -> p (a b)").bitcast(F32)
        row_scales = k_st[0][:, :, :].rearrange("p a b -> p (a b)").bitcast(F32)\
            .rearrange("p (e d) -> p e d", e=E)
        g_ring = w_hi[:, :, :, :].rearrange("p n c m -> p (n c) m").bitcast(F32)[:, 0:RING, :]
        g_rows = [g_ring[:, i, :] for i in range(RING)]
        iota_expert = iota_lane[:, 0:E]
        e_htf = [ht[:, :, 0:P], ht[:, :, P:2 * P]]
        e_hth = [ht_hi[:, :, 0:P], ht_hi[:, :, P:2 * P]]
        e_htl = [ht_lo[:, :, 0:P], ht_lo[:, :, P:2 * P]]
        e_up = [x1[:, 0:2, :].rearrange("p a b -> p (a b)"), x2[:, 0:2, :].rearrange("p a b -> p (a b)")]
        e_tanh = [xb[:, :, :].rearrange("p a b -> p (a b)"), c_in[:, :, :].rearrange("p a b -> p (a b)")]
        e_gate = [o_sb[:, 0, :], o_sb[:, 1, :]]
        e_gh = [k_stage[0][:, 0, :], k_stage[0][:, 1, :]]
        e_gl = [k_stage[1][:, 0, :], k_stage[1][:, 1, :]]
        e_yv = [w_raw[:, 0:D], w_raw[:, D:2 * D]]
        OE = [O[:, 0:D], FB[1][:, 0:D]]
        e_res = [w_raw[:, 2 * D:3 * D], w_raw[:, 3 * D:4 * D]]

        @block.sync
        def _(sp):
            sp.dma_start(c_in[:, :, :], c_v[0]).then_inc(c_loaded, 16)
            sp.dma_start(x_in[:, :, :], x_v[0]).then_inc(x_loaded, 16)
            for n, w in ((WV2, wv2), (WQ, wq1), (WK1, wk1), (WK2, wk2), (WV1, wv1)):
                sp.dma_start(landing[n].rearrange("p (c n) -> p c n", c=DC),
                             w.rearrange("(c p) n -> p c n", p=P)).then_inc(weights_in[n], 16)
            sp.dma_start(raw_up, sw1.rearrange("(c p) d -> p c d", p=P)).then_inc(raw_loaded, 16)
            sp.dma_start(landing[5].rearrange("p (c n) -> p c n", c=IC),
                         wo.rearrange("(c p) n -> p c n", p=P)).then_inc(weights_in[5], 16)
            sp.dma_start(rw_raw, router_w).then_inc(rw_in, 16)
            sp.dma_start(bo_raw, bo.rearrange("(a n) -> a n", a=1)).then_inc(bo_in, 16)
            sp.dma_start(gb[:, 0, :], gamma.rearrange("(c p) -> p c", p=P), allow_slow_non_contiguous=True).then_inc(gb_in, 16)
            sp.dma_start(gb[:, 1, :], beta.rearrange("(c p) -> p c", p=P), allow_slow_non_contiguous=True).then_inc(gb_in, 16)
            sp.dma_start(xb[:, :, :], x_v[0]).then_inc(xr_loaded, 16)

            def body(b, par, e):
                f, t, fp = b + 1, b - 1, 1 - par
                if has_front(b) and not (is_static(b) and b == -1):
                    at_least(sp, tern_ready, f + SHARED_Q)
                    src = (ew1_v if fp == 0 else ew2_v)[bass.ds(e, 1)].rearrange("e p c d -> p (e c) d")
                    sp.dma_start(raw_up if fp == 0 else raw_down, src).then_inc(raw_loaded, 16)
                if has_front(b):
                    if not is_static(b) or f + 1 < B:
                        nb = bass.ds(f + 1, 1)
                        sp.wait_ge(f_full, f * FRONT + FC_CTX + 1)
                        sp.dma_start(c_in[:, :, :], c_v[nb].rearrange("b p t d -> p (b t) d")).then_inc(c_loaded, 16)
                        sp.wait_ge(x1_ready, f + 1)
                        sp.dma_start(x_in[:, :, :], x_v[nb].rearrange("b p t d -> p (b t) d")).then_inc(x_loaded, 16)
                if has_down(b):
                    sp.wait_ge(r_ready, b - 1)
                    sp.dma_start(rows_v[bass.ds(b - 2, 1)].rearrange("b p t d -> p (b t) d"), row[:, :, :])\
                        .then_inc(rows_stored, 16)
                if has_front(b):
                    for s in range(2):
                        sp.wait_ge(f_lo, f * SPLIT + Q0 + s + 1)
                        for odd in range(2):
                            for half in range(2):
                                sp.dma_start(q_st[fp][half * DH:(half + 1) * DH, 4 * s + odd:4 * s + odd + 3:2, :, :],
                                             q_stage[s][odd * DH:(odd + 1) * DH, :, :, :]).then_inc(q_stacked[s], 16)
                    for c in range(IC):
                        sp.wait_ge(f_lo, f * SPLIT + K0 + c + 1)
                        for odd in range(2):
                            for half in range(2):
                                sp.dma_start(k_st[fp][half * DH:(half + 1) * DH, 2 * c + odd, :],
                                             k_stage[c % 3][odd * DH:(odd + 1) * DH, half, :])\
                                    .then_inc(k_stacked[c], 16)
                if has_tail(b):
                    if not is_static(b) or t + 1 < B:
                        sp.wait_ge(x2_ready, t * 2 + 2)
                        sp.dma_start(xb[:, :, :], x_v[bass.ds(t + 1, 1)].rearrange("b p t d -> p (b t) d"))\
                            .then_inc(xr_loaded, 16)

            slots(sp, body)

        @block.gpsimd
        def _(pool):
            g = nc.gpsimd
            g.memset(ident[:, :], 0.0).then_inc(const_ready, 1)
            g.memset(ident16[:, :], 0.0).then_inc(const_ready, 1)
            g.memset(below16[:, :], 1.0).then_inc(const_ready, 1)
            g.memset(ones[:, :], 1.0).then_inc(const_ready, 1)
            g.memset(ones16[:, :], 1.0).then_inc(const_ready, 1)
            g.memset(minus_half[:, :], -0.5).then_inc(const_ready, 1)
            pool.wait_ge(const_ready, 6)
            for m in (ident, ident16):
                g.affine_select(out=m[:, :], in_=m[:, :], compare_op=ALU.not_equal, fill=1.0, base=0,
                                pattern=[[-1, P]], channel_multiplier=1).then_inc(const_ready, 1)
            g.affine_select(out=below16[:, :], in_=below16[:, :], compare_op=ALU.is_gt, fill=0.0, base=0,
                            pattern=[[1, P]], channel_multiplier=-1).then_inc(const_ready, 1)

            def number_lines():
                pool.wait_ge(x1_ready, B)
                g.iota(iota_lane, [[1, P]], base=0, channel_multiplier=0,
                       allow_small_or_imprecise_dtypes=True).then_inc(iota_ready, 1)
                g.iota(iota_tile, [[1, SLOTS]], base=0, channel_multiplier=0,
                       allow_small_or_imprecise_dtypes=True).then_inc(iota_ready, 1)
                g.iota(iota_tiles128, [[P, TILES]], base=0, channel_multiplier=0,
                       allow_small_or_imprecise_dtypes=True).then_inc(iota_ready, 1)
                g.iota(iota_tile1, [[1, TILES]], base=1, channel_multiplier=0,
                       allow_small_or_imprecise_dtypes=True).then_inc(iota_ready, 1)
                g.iota(iota_down, [[-1, E]], base=E, channel_multiplier=0,
                       allow_small_or_imprecise_dtypes=True).then_inc(iota_ready, 1)
                g.iota(iota_p, [[1, 1]], base=0, channel_multiplier=1,
                       allow_small_or_imprecise_dtypes=True).then_inc(iota_ready, 1)
                g.memset(ones32, 1.0).then_inc(iota_ready, 1)
                pool.wait_ge(f_lo, B * SPLIT)
                g.memset(g_ring, 0.0).then_inc(zeroed, 1)

            def body(b, par, e):
                f, t, fp = b + 1, b - 1, 1 - par
                if has_front(b):
                    pool.wait_ge(ve1_ready, f * 2 + 2)
                    g.tensor_tensor(rs1[:, :], ve1[:, :], minus_half[:, :], ALU.pow).then_inc(rs1_ready, 1)
                    pool.wait_ge(rs1_ready, f + 1)
                    g.tensor_tensor(shift1[:, :], neg_mean1[:, :], rs1[:, :], ALU.mult).then_inc(shift1_ready, 1)
                def ternary():
                    n = matrix_of(f)
                    pool.wait_ge(sign_ready, n * 2 + 2)
                    g.tensor_tensor(above[:, :], above[:, :], under[:, :], ALU.subtract).then_inc(tern_ready, 1)

                if is_static(b) and b == -1:
                    pool.wait_ge(tern_ready, 1)
                    g.dma_start(out=raw_up, in_=ew1_v[0]).then_inc(raw_by_pool, 16)
                if has_front(b) and not has_tail(b):
                    ternary()
                if is_static(b) and b == -1:
                    pool.wait_ge(tern_ready, 2)
                    g.dma_start(out=raw_down, in_=sw2.rearrange("(c p) f -> p c f", p=P)).then_inc(raw_by_pool, 16)
                if has_down(b):
                    pool.wait_ge(shared_ready, b - 1)
                    g.tensor_tensor(row[:, :, 0:D], row[:, :, 0:D], x2[:, :, :], ALU.add).then_inc(r_ready, 1)
                if is_static(b) and b == B:
                    number_lines()
                if has_tail(b):
                    pool.wait_ge(xr_loaded, (t + 1) * 16)
                    if is_static(b) and b == 1:
                        pool.wait_ge(prep_free, PREP)
                    g.tensor_tensor(xb[:, :, :], xb[:, :, :], bo_row[:, :].unsqueeze(1).broadcast_to([P, TB, D]),
                                    ALU.add).then_inc(xb_ready, 1)
                    pool.wait_ge(ve2_ready, t * 2 + 2)
                    g.tensor_tensor(rs2[:, :], ve2[:, :], minus_half[:, :], ALU.pow).then_inc(rs2_ready, 1)
                    pool.wait_ge(rs2_ready, t + 1)
                    g.tensor_tensor(shift2[:, :], neg_mean2[:, :], rs2[:, :], ALU.mult).then_inc(shift2_ready, 1)
                    pool.wait_ge(h_hi_ready, t + 1)
                    g.tensor_tensor(ht_lo[:, :, :], ht[:, :, :], ht_hi[:, :, :], ALU.subtract).then_inc(h_lo_ready, 1)
                    if has_front(b):
                        ternary()
                    for j in range(2):
                        pool.wait_ge(gate_ready, t * 2 + j + 1)
                        sc = up_scale[:, E, 2 * j:2 * j + 2].unsqueeze(2).broadcast_to([P, 2, T])
                        g.tensor_tensor(gate[j][:, :, :], gate[j][:, :, :], sc, ALU.mult).then_inc(gated, 1)
                        pool.wait_ge(g_hi_ready, t * 2 + j + 1)
                        g.tensor_tensor(g_lo[:, 2 * j:2 * j + 2, :], gate[j][:, :, :], g_hi[:, 2 * j:2 * j + 2, :],
                                        ALU.subtract).then_inc(g_lo_ready, 1)

            slots(pool, body)

            pool.wait_ge(rows_stored, 16 * B)
            pool.wait_ge(zeroed, 1)
            pool.wait_ge(table_ready, 1)

            def gather(a):
                if a >= RING:
                    pool.wait_ge(e_out, a - RING + 1)
                g.indirect_dma_start(out=g_rows[a % RING], out_offset=None, in_=rows,
                                     in_offset=bass.IndirectOffsetOnAxis(ap=slot_idx[:, a:a + 1], axis=0),
                                     bounds_check=B * T - 1, oob_is_err=False).then_inc(gathered[a % RING], 16)

            for a in range(RING):
                gather(a)
            for a in range(SLOTS):
                pool.wait_ge(e_y, a + 1)
                if a >= 2:
                    pool.wait_ge(stored[a % 2], 16 * (a // 2))
                g.tensor_tensor(e_res[a % 2], e_yv[a % 2], g_rows[a % RING][:, 0:D], ALU.add).then_inc(e_out, 1)
                pool.wait_ge(e_out, a + 1)
                g.indirect_dma_start(out=out, out_offset=bass.IndirectOffsetOnAxis(ap=slot_idx[:, a:a + 1], axis=0),
                                     in_=e_res[a % 2], in_offset=None,
                                     bounds_check=B * T - 1, oob_is_err=False).then_inc(stored[a % 2], 16)
                if a + RING < SLOTS:
                    gather(a + RING)
            for i in range(2):
                pool.wait_ge(stored[i], 16 * (SLOTS // 2))

        @block.scalar
        def _(act):
            a_ = nc.scalar.activation
            def weight_hi(n):
                act.wait_ge(weights_in[n], 16)
                if n < 5:
                    a_(w_hi[:, n, :, :], landing[n].rearrange("p (c n) -> p c n", c=DC), ACT.Copy,
                       scale=QSCALE if n == WQ else 1.0).then_inc(w_hi_ready, 1)
                else:
                    a_(wo_hi[:, :, :], landing[5].rearrange("p (c n) -> p c n", c=IC), ACT.Copy).then_inc(w_hi_ready, 1)

            def ternary_move(full, e, down, src, done):
                act.wait_ge(*full)
                if down:
                    dst = down16[:, bass.ds(e, 1), :, :].rearrange("p a c d -> p (a c d)")
                else:
                    dst = up16[:, bass.ds(e, 1), :, :].rearrange("p a c f -> p (a c f)")
                a_(dst, src, ACT.Copy).then_inc(done, 1)

            def prep_act(j):
                if j == SHARED_UP:
                    ternary_move((prep_full, j + 1), E, False, tb16, prep_free)
                elif j == ROUTER_W:
                    act.wait_ge(prep_full, j + 1)
                    tbr = TBK[:, 0:DC * E].rearrange("p (c e) -> p c e", c=DC)
                    a_(rw_hi[:, :, :], tbr, ACT.Copy, scale=RSCALE).then_inc(rw_hi_ready, 1)
                elif j == BIAS:
                    act.wait_ge(prep_full, j + 1)
                    a_(bo_row[:, :], TBK[:, 0:D], ACT.Copy).then_inc(prep_free, 1)
                elif j == SHARED_DOWN:
                    ternary_move((prep_full, j + 1), E, True, tb16, prep_free)
                else:
                    act.wait_ge(prep_full, j + 1)
                    a_(shared_row[:, :], TBK[:, 0:D], ACT.Copy).then_inc(prep_free, 1)
                    act.wait_ge(gb_in, 32)
                    act.wait_ge(half_up_ready, 1)

            def front_hi(b, par, e, j):
                f, fp = b + 1, 1 - par
                k = (j + fp) % 2
                if j == QUANT:
                    ternary_move((f_full, f * FRONT + QUANT + 1), e, fp == 1, fb16[k], tern_moved)
                    return
                act.wait_ge(f_full, f * FRONT + j + 1)
                if j in (FC_CTX, FC_X):
                    lo = T if j == FC_CTX else 0
                    a_(xt_hi[:, :, lo:lo + T], fb2[k], ACT.Copy).then_inc(f_hi, 1)
                elif j in (V0, V1, V2, V3):
                    jb = {V0: 0, V1: 1, V2: 2, V3: 3}[j]
                    a_(v_st[fp][:, 0, jb, :, 0:DH], fb_heads[k], ACT.Copy).then_inc(f_hi, 1)
                elif j in (Q0, Q1):
                    at_least(act, q_stacked[j - Q0], f * 64)
                    a_(q_stage[j - Q0][:, :, 0, :], fb2[k], ACT.Copy).then_inc(f_hi, 1)
                else:
                    c = j - K0
                    if c == 3:
                        act.wait_ge(k_stacked[0], f * 64 + 64)
                    else:
                        at_least(act, k_stacked[3 if c == 0 else c], f * 64)
                    a_(k_stage[c % 3][:, 0, :], FB[k][:, :], ACT.Copy).then_inc(f_hi, 1)

            def normalise(dst, src, rs, shift, done):
                for i in range(TB):
                    last = a_(dst[i], src[:, i, :], ACT.Identity, bias=shift[:, i:i + 1], scale=rs[:, i:i + 1])
                last.then_inc(done, 1)

            def normalise_front(b):
                act.wait_ge(shift1_ready, b + 2)
                at_least(act, f_hi, (b + 1) * SPLIT)
                normalise([x1[:, 0, :], x1[:, 1, :]], x_in, rs1, shift1, x1_ready)

            def layernorm_tail(b):
                t = b - 1
                act.wait_ge(shift2_ready, t + 1)
                at_least(act, rows_stored, t * 16)
                normalise([row[:, 0, D:2 * D], row[:, 1, D:2 * D]], x2, rs2, shift2, hn_ready)

            def gate_hi(b, n):
                t = b - 1
                act.wait_ge(gated, t * 2 + n + 1)
                a_(g_hi[:, 2 * n:2 * n + 2, :], gate[n][:, :, :], ACT.Copy).then_inc(g_hi_ready, 1)

            def row_sums(n, down):
                cols, width = (DC, FW) if down else (FC, D)
                if is_static(n) and n < 3:
                    act.wait_ge(*((raw_by_pool, n * 16) if n else (raw_loaded, 16)))
                else:
                    act.wait_ge(raw_loaded, (n - 1) * 16)
                at_least(act, tern_ready, n)
                for c in range(cols):
                    last = a_(under[:, c * width:(c + 1) * width], (raw_down if down else raw_up)[:, c, :], ACT.Abs,
                              accum_out=w_abs[:, c:c + 1])
                last.then_inc(abs_ready, 1)

            def tail_act(b, j):
                t = b - 1
                if j in (OT0, OT1):
                    act.wait_ge(t_full, t * TAIL + j + 1)
                    a_(ot_hi[:, :, :], TBK[:, :].rearrange("p (c t) -> p c t", c=IC), ACT.Copy)\
                        .then_inc(ot_hi_ready, 1)
                elif j == HT:
                    act.wait_ge(t_full, t * TAIL + j + 1)
                    for c in range(DC):
                        last = a_(ht[:, c, :], tb2[:, c, :], ACT.Identity, bias=gb[:, 1, c:c + 1], scale=gb[:, 0, c:c + 1])
                    last.then_inc(ht_ready, 1)
                    act.wait_ge(ht_ready, t + 1)
                    a_(ht_hi[:, :, :], ht[:, :, :], ACT.Copy).then_inc(h_hi_ready, 1)
                elif j in (UP0, UP1):
                    act.wait_ge(t_full, t * TAIL + j + 1)
                    for c in range(2):
                        n = 2 * (j - UP0) + c
                        last = a_(th[:, c, :], tb2[:, c, :], ACT.Tanh, scale=half_up[:, n:n + 1])
                    last.then_inc(th_ready, 1)

            def body(b, par, e):
                for u in units_of(b):
                    g = b * UNITS + u
                    if is_static(b) and b == B and u == HT_AT + 3:
                        act.wait_ge(dve_step, 2)
                        a_(exps, exps, ACT.Exp, scale=1.0 / RSCALE).then_inc(exps_ready, 1)
                    if has_tail(b) and u - 1 in TAIL_AT:
                        tail_act(b, TAIL_AT[u - 1])
                    if has_front(b) and u - 1 in FRONT_AT:
                        front_hi(b, par, e, FRONT_AT[u - 1])
                    if has_attention(b) and u == 0:
                        front_hi(b - 1, 1 - par, e, V1)
                    if is_static(b) and b <= 0 and u - 1 in PREP_AT[b]:
                        prep_act(PREP_AT[b][u - 1])
                    if is_static(b) and b == -1 and u < 6:
                        weight_hi(u)
                    if is_static(b) and b <= 0:
                        for n in {(-1, 5): (0,), (-1, 10): (1,), (0, 1): (2,), (0, 6): (3,)}.get((b, u), ()):
                            row_sums(n, n > 1)
                    if (has_attention(b) and not (is_static(b) and b == 0 and u == 0)) or (is_static(b) and b == B and u == 0):
                        act.wait_ge(pt_ready, g)
                        if not (is_static(b) and b == 0 and u < 3):
                            act.wait_ge(pv_done, g - 2)
                        a_(pt_hi[(u + 1) % 2][:, :, :], PT[(u + 1) % 2][:, :].rearrange("p (k i) -> p k i", k=KB),
                           ACT.Copy).then_inc(pt_hi_ready, 1)
                    if has_attention(b):
                        act.wait_ge(max_ready, g + 1)
                        if not (is_static(b) and b == 0 and u < 2):
                            act.wait_ge(pt_ready, g - 1)
                        a_(probs[u % 2][:, :], S[u % 2][:, :], ACT.Exp, bias=neg_max[:, u % 4:u % 4 + 1],
                           accum_out=sums[:, u:u + 1])\
                            .then_inc(probs_ready, 1)
                    if has_front(b) and u == SUMS_AT and not (is_static(b) and b <= 0):
                        row_sums(matrix_of(b + 1), par == 0)
                    if has_front(b) and u == NORM_X_AT:
                        normalise_front(b)
                    if has_tail(b) and u == NORM_H_AT:
                        layernorm_tail(b)
                    if has_tail(b) and u in GATE_HI_AT:
                        gate_hi(b, GATE_HI_AT[u])
                    if has_down(b) and u == 0:
                        gate_hi(b - 1, 1)

            slots(act, body)

            for n in range(4):
                act.wait_ge(rowscale_full, n + 1)
                a_(row_scales[:, 2 * n:2 * n + 2, :], FB[0][:, :].rearrange("p (e d) -> p e d", e=2), ACT.Copy)\
                    .then_inc(rowscale_free, 1)

            def split_ht(a, s):
                act.wait_ge(e_ht_full, a + 1)
                v = S[s][:, 0:DC * P].rearrange("p (c t) -> p c t", c=DC)
                if not (is_static(a) and a < 2):
                    act.wait_ge(e_ht_lo, a - 1)
                for c in range(DC):
                    last = a_(e_htf[s][:, c, :], v[:, c, :], ACT.Identity, bias=gb[:, 1, c:c + 1], scale=gb[:, 0, c:c + 1])
                last.then_inc(e_ht, 1)
                act.wait_ge(e_ht, a + 1)
                if not (is_static(a) and a < 2):
                    act.wait_ge(e_up_full, a - 1)
                a_(e_hth[s], e_htf[s], ACT.Copy).then_inc(e_ht_hi, 1)

            def tanh(a, s):
                act.wait_ge(e_u, a + 1)
                a_(e_tanh[s], e_up[s], ACT.Tanh, scale=1.0 / HSCALE).then_inc(e_th, 1)

            def gate_hi(a, s):
                act.wait_ge(e_g, a + 1)
                if not (is_static(a) and a < 2):
                    act.wait_ge(e_down_full, a - 1)
                a_(e_gh[s], e_gate[s], ACT.Copy).then_inc(e_g_hi, 1)

            def step(k, r, n, expert):
                if tile_in_range(k - 1):
                    gate_hi(k - 1, (r + 1) % 2)
                if tile_in_range(k):
                    tanh(k, r % 2)
                if tile_in_range(k + 2):
                    split_ht(k + 2, r % 2)

            tiles(act, step)

        @block.vector
        def _(dve):
            v = nc.vector
            def weight_lo(n):
                dve.wait_ge(w_hi_ready, n + 1)
                if n < 5:
                    v.scalar_tensor_tensor(w_lo[:, n, :, :].rearrange("p c n -> p (c n)"), landing[n],
                                           QSCALE if n == WQ else 1.0,
                                           w_hi[:, n, :, :].rearrange("p c n -> p (c n)").bitcast(F32),
                                           ALU.mult, ALU.subtract).then_inc(w_lo_ready, 1)
                else:
                    v.tensor_tensor(wo_lo[:, :, :], landing[5].rearrange("p (c n) -> p c n", c=IC),
                                    wo_hi[:, :, :].bitcast(F32), ALU.subtract).then_inc(w_lo_ready, 1)

            def quantise(n, e, down, stage):
                cols, width = (DC, FW) if down else (FC, D)
                raw = raw_down if down else raw_up
                if stage == 0:
                    row_scale(n, e, cols, width, raw, down)
                    return
                if stage == 1:
                    dve.wait_ge(half_ready, n * 3 + 3)
                    if is_static(n) and n < 4:
                        at_least(dve, f_full if n == 2 else prep_full, (0, SHARED_UP + 1, QUANT + 1, SHARED_DOWN + 1)[n])
                    else:
                        dve.wait_ge(f_full, (n - 3) * FRONT + QUANT + 1)
                if stage < 3:
                    side = w_half[:, stage - 1, 0:cols].unsqueeze(2).broadcast_to([P, cols, 1024 // cols])
                    dst = (above, under)[stage - 1][:, :].rearrange("p (c d) -> p c d", c=cols)
                    v.tensor_tensor(dst, raw, side, ALU.is_gt if stage == 1 else ALU.is_lt).then_inc(sign_ready, 1)
                    return
                dve.wait_ge(sign_ready, n * 2 + 2)
                v.tensor_tensor(above[:, :], above[:, :], under[:, :], ALU.subtract).then_inc(tern_ready, 1)

            def row_scale(n, e, cols, width, raw, down):
                dve.wait_ge(abs_ready, n + 1)
                v.tensor_scalar(w_abs[:, 0:cols], w_abs[:, 0:cols], 1.0 / width, EPS, ALU.mult, ALU.max)\
                    .then_inc(scale_ready, 1)
                dve.wait_ge(scale_ready, n + 1)
                v.tensor_scalar(w_half[:, 0, 0:cols], w_abs[:, 0:cols], 0.5, None, ALU.mult).then_inc(half_ready, 1)
                v.tensor_scalar(w_half[:, 1, 0:cols], w_abs[:, 0:cols], -0.5, None, ALU.mult).then_inc(half_ready, 1)
                dst = (down_scale if down else up_scale)[:, bass.ds(e, 1), 0:cols].rearrange("p a c -> p (a c)")
                v.tensor_scalar(dst, w_abs[:, 0:cols], 1.0 / HSCALE if down else HSCALE / 2, None, ALU.mult)\
                    .then_inc(half_ready, 1)
                if is_static(n) and n == 0:
                    v.tensor_scalar(half_up[:, :], w_abs[:, :], 0.5, None, ALU.mult).then_inc(half_up_ready, 1)

            def prep_dve(b, u):
                if b == -1:
                    if u < 6:
                        weight_lo(u)
                    if PREP_AT[-1].get(u - 1) == ROUTER_W:
                        dve.wait_ge(rw_hi_ready, 1)
                        v.scalar_tensor_tensor(rw_lo[:, :, :].rearrange("p c e -> p (c e)"), TBK[:, 0:DC * E], RSCALE,
                                               rw_hi[:, :, :].rearrange("p c e -> p (c e)"), ALU.mult, ALU.subtract)\
                            .then_inc(prep_free, 1)
                    for stage in {5: (0,), 6: (1,), 7: (2, 3)}.get(u, ()):
                        quantise(0, E, False, stage)
                    for stage in {10: (0,), 11: (1,), 12: (2,)}.get(u, ()):
                        quantise(1, 0, False, stage)
                else:
                    for stage in {1: (0,), 2: (1,), 3: (2, 3)}.get(u, ()):
                        quantise(2, E, True, stage)
                    if u == 4:
                        dve.wait_ge(half_ready, 9)
                        for c in range(DC):
                            v.tensor_scalar(diag[:, c, :], ident[:, :], down_scale[:, E, c:c + 1], None, ALU.mult)\
                                .then_inc(diag_ready, 1)
                    for stage in {6: (0,), 8: (1,), 12: (2,)}.get(u, ()):
                        quantise(3, 0, True, stage)

            def settle(s, value):
                dve.wait_ge(s, value)
                v.memset(pause[:, :], 0.0)

            def stats_front(b):
                f = b + 1
                dve.wait_ge(x_loaded, (f + 1) * 16)
                for i in range(TB):
                    v.bn_stats(st1[:, i, :], x_in[:, i, :]).then_inc(stats1, 1)

            def variance_front(b):
                f = b + 1
                settle(stats1, f * 2 + 2)
                for i in range(TB):
                    v.bn_aggr(mv1[:, i, :], st1[:, i, :]).then_inc(var1, 1)
                dve.wait_ge(var1, f * 2 + 2)
                v.tensor_scalar(ve1[:, :], mv1[:, :, 1], EPS, None, ALU.add).then_inc(ve1_ready, 1)
                v.tensor_scalar(neg_mean1[:, :], mv1[:, :, 0], -1.0, None, ALU.mult).then_inc(ve1_ready, 1)

            def front_lo(b, par, j):
                f, fp = b + 1, 1 - par
                k = (j + fp) % 2
                if j == QUANT:
                    return
                n = j - (j > QUANT)
                dve.wait_ge(f_hi, f * SPLIT + n + 1)
                if j in (FC_CTX, FC_X):
                    lo = T if j == FC_CTX else 0
                    v.tensor_tensor(xt_lo[:, :, lo:lo + T], fb2[k], xt_hi[:, :, lo:lo + T].bitcast(F32), ALU.subtract)\
                        .then_inc(f_lo, 1)
                elif j in (V0, V1, V2, V3):
                    jb = {V0: 0, V1: 1, V2: 2, V3: 3}[j]
                    v.tensor_tensor(v_st[fp][:, 1, jb, :, 0:DH], fb_heads[k], v_st[fp][:, 0, jb, :, 0:DH], ALU.subtract)\
                        .then_inc(f_lo, 1)
                elif j in (Q0, Q1):
                    s = j - Q0
                    v.tensor_tensor(q_stage[s][:, :, 1, :], fb2[k], q_stage[s][:, :, 0, :], ALU.subtract).then_inc(f_lo, 1)
                else:
                    s = (j - K0) % 3
                    v.tensor_tensor(k_stage[s][:, 1, :], FB[k][:, :], k_stage[s][:, 0, :], ALU.subtract).then_inc(f_lo, 1)

            def normalise_heads(n, k):
                o4 = O[:, (k % 2) * 4 * DH:(k % 2 + 1) * 4 * DH].rearrange("p (h d) -> p h d", h=4)
                dve.wait_ge(pv_done, (n + 1) * 4)
                v.reciprocal(inv_sum[:, :], sums[:, 4 * k:4 * k + 4]).then_inc(inv_ready, 1)
                dve.wait_ge(inv_ready, n + 1)
                dst = o_sb[:, k // 2, (k % 2) * 4 * DH:(k % 2 + 1) * 4 * DH].rearrange("p (h d) -> p h d", h=4)
                v.tensor_tensor(dst, o4[:, :, 0:DH], inv_sum[:, :].unsqueeze(2).broadcast_to([P, 4, DH]), ALU.mult)\
                    .then_inc(normed, 1)

            def logits_out(t, full, src):
                if full is not None:
                    dve.wait_ge(t_full, full)
                v.tensor_copy(logits[:, bass.ds(t * TB, TB), :], src[:, D:D + TB * E].rearrange("p (t e) -> p t e", e=E))\
                    .then_inc(logits_ready, 1)

            def tail_dve(b, j):
                t = b - 1
                if j in (OT0, OT1):
                    dve.wait_ge(ot_hi_ready, t * 2 + (j == OT1) + 1)
                    v.tensor_tensor(ot_lo[:, :, :], TBK[:, :].rearrange("p (c t) -> p c t", c=IC),
                                    ot_hi[:, :, :].bitcast(F32), ALU.subtract).then_inc(ot_lo_ready, 1)
                elif j in (WO0, WO1):
                    i = int(j == WO1)
                    dve.wait_ge(t_full, t * TAIL + j + 1)
                    if i == 0:
                        dve.wait_ge(xb_ready, t + 1)
                        at_least(dve, r_ready, t)
                    v.tensor_tensor(x2[:, i, :], TBK[:, 0:D], xb[:, i, :], ALU.add).then_inc(x2_ready, 1)
                    if j == WO0 and not (is_static(t) and t == 0):
                        logits_out(t - 1, t * TAIL + j + 1, TBK)
                elif j in (UP0, UP1):
                    n = j - UP0
                    dve.wait_ge(th_ready, t * 2 + n + 1)
                    v.scalar_tensor_tensor(gate[n][:, :, :].rearrange("p c t -> p (c t)"),
                                           th[:, :, :].rearrange("p c t -> p (c t)"), 1.0, TBK[:, :],
                                           ALU.add, ALU.mult).then_inc(gate_ready, 1)
                elif j == DOWN:
                    dve.wait_ge(t_full, t * TAIL + j + 1)
                    v.tensor_tensor(row[:, :, 0:D], tb2, shared_row[:, :].unsqueeze(1).broadcast_to([P, TB, D]),
                                    ALU.mult).then_inc(shared_ready, 1)

            def residual_stats(b, j):
                t = b - 1
                if j in (WO0, WO1):
                    i = int(j == WO1)
                    dve.wait_ge(x2_ready, t * 2 + i + 1)
                    v.bn_stats(st2[:, i, :], x2[:, i, :]).then_inc(stats2, 1)
                    settle(stats2, t * 2 + i + 1)
                    v.bn_aggr(mv2[:, i, :], st2[:, i, :]).then_inc(var2, 1)
                    if i == TB - 1:
                        dve.wait_ge(var2, t * 2 + 2)
                        v.tensor_scalar(ve2[:, :], mv2[:, :, 1], 1.0 + EPS, EPS * EPS, ALU.mult, ALU.add)\
                            .then_inc(ve2_ready, 1)
                        v.tensor_scalar(neg_mean2[:, :], mv2[:, :, 0], -1.0, None, ALU.mult).then_inc(ve2_ready, 1)

            step = [0]

            def then(ins):
                step[0] += 1
                ins.then_inc(dve_step, 1)
                dve.wait_ge(dve_step, step[0])

            def spread(ap, shape, axis):
                return ap.unsqueeze(axis).broadcast_to(shape)

            TE = [P, TILES, E]

            def choose_experts():
                dve.wait_ge(logits_ready, B)
                dve.wait_ge(iota_ready, 7)
                then(v.tensor_reduce(top, logits[:, :, :], AX.X, ALU.max))
                then(v.tensor_tensor(exps, logits[:, :, :], spread(top, TE, 2), ALU.subtract))
                then(v.tensor_tensor(score_e, logits[:, :, :], spread(top, TE, 2), ALU.is_equal))
                then(v.tensor_tensor(score_e, score_e, spread(iota_down, TE, 1), ALU.mult))
                then(v.tensor_reduce(top, score_e, AX.X, ALU.max))
                then(v.tensor_tensor(hot, score_e, spread(top, TE, 2), ALU.is_equal))
                v.tensor_copy(hot16, hot).then_inc(onehot_ready, 1)

            def count_tokens():
                dve.wait_ge(exps_ready, 1)
                then(v.tensor_reduce(esum, exps, AX.X, ALU.add))
                then(v.reciprocal(prob, esum))
                then(v.tensor_copy(p_hi, prob))
                then(v.tensor_tensor(p_lo, prob, p_hi, ALU.subtract))
                dve.wait_ge(ranks_ready, 1)
                then(v.tensor_copy(counts, S[1][:, 0:TILES * E].rearrange("p (t e) -> p t e", e=E)))
                for e in range(E):
                    last = v.tensor_tensor_scan(incl[:, :, e], ones32, counts[:, :, e], 0.0, ALU.mult, ALU.add)
                then(last)
                then(v.tensor_copy(total, incl[:, TILES - 1, :]))

            def place_tokens():
                then(v.tensor_tensor(steps32, spread(total, [P, E, TILES], 2), spread(iota_tiles128, [P, E, TILES], 1),
                                     ALU.is_gt))
                then(v.tensor_reduce(tiles_of, steps32, AX.X, ALU.add))
                then(v.tensor_tensor_scan(tile_end, ones32[:, 0:E], tiles_of, 0.0, ALU.mult, ALU.add))
                then(v.tensor_tensor(base, tile_end, tiles_of, ALU.subtract))
                then(v.tensor_scalar(base, base, float(P), None, ALU.mult))
                then(v.tensor_tensor(place, incl, counts, ALU.subtract))
                then(v.tensor_tensor(place, place, S[0][:, 0:TILES * E].rearrange("p (t e) -> p t e", e=E), ALU.add))
                then(v.tensor_tensor(place, place, spread(base, TE, 1), ALU.add))
                then(v.tensor_tensor(place, place, hot, ALU.mult))
                then(v.tensor_reduce(dest, place, AX.X, ALU.add))
                then(v.tensor_copy(desti, dest))
                then(v.tensor_scalar(tilei, desti, 7, None, ALU.arith_shift_right))
                then(v.tensor_scalar(lanei, desti, P - 1, None, ALU.bitwise_and))
                then(v.tensor_copy(slot_tile, tilei))
                then(v.tensor_copy(lane, lanei))

            def table():
                TL, TA = [P, TILES, P], [P, TILES, SLOTS]
                then(v.tensor_tensor(lane_hot, spread(iota_lane, TL, 1), spread(lane, TL, 2), ALU.is_equal))
                then(v.tensor_tensor(tile_hot, spread(iota_tile, TA, 1), spread(slot_tile, TA, 2), ALU.is_equal))
                v.tensor_tensor(map_ids[:, :, 0, :], tile_hot, spread(iota_tile1, TA, 2), ALU.mult).then_inc(maps_ready, 1)
                v.tensor_scalar(map_ids[:, :, 1, :], tile_hot, iota_p, None, ALU.mult).then_inc(maps_ready, 1)
                v.tensor_tensor(map_probs[:, :, 0, :], tile_hot, spread(p_hi, TA, 2), ALU.mult).then_inc(maps_ready, 1)
                v.tensor_tensor(map_probs[:, :, 1, :], tile_hot, spread(p_lo, TA, 2), ALU.mult).then_inc(maps_ready, 1)
                EA = [P, SLOTS, E]
                then(v.tensor_tensor(owner, spread(tile_end, EA, 1), spread(iota_tile, EA, 2), ALU.is_le))
                then(v.tensor_reduce(tile_e, owner, AX.X, ALU.add))
                then(v.tensor_scalar(tile_e, tile_e, float(E - 1), None, ALU.min))
                then(v.tensor_copy(tile_ei, tile_e))
                v.tensor_tensor(diag_all.rearrange("p (n k) -> p n k", k=P), spread(ident[:, :], [P, E * DC, P], 1),
                                spread(down_scale[:, 0:E, :].rearrange("p e c -> p (e c)"), [P, E * DC, P], 2),
                                ALU.mult).then_inc(dmat_ready, 1)
                dve.wait_ge(slots_ready, 1)
                q_ = TBK[:, 0:2 * SLOTS]
                then(v.tensor_scalar(absent, q_[:, 0:SLOTS], 0.5, float(ABSENT), ALU.is_lt, ALU.mult))
                then(v.scalar_tensor_tensor(slot_id, q_[:, 0:SLOTS], float(P), absent, ALU.mult, ALU.add))
                then(v.tensor_tensor(slot_id, slot_id, q_[:, SLOTS:2 * SLOTS], ALU.add))
                then(v.tensor_scalar(slot_id, slot_id, float(P), None, ALU.subtract))
                then(v.tensor_copy(slot_prob, TBK[:, 2 * SLOTS:3 * SLOTS]))
                then(v.tensor_tensor(slot_prob, slot_prob, TBK[:, 3 * SLOTS:4 * SLOTS], ALU.add))
                v.tensor_copy(slot_idx, slot_id).then_inc(table_ready, 1)

                then(v.tensor_tensor(owner, spread(tile_e, EA, 2), spread(iota_expert, EA, 1), ALU.is_equal))
                for c in range(FC):
                    last = v.tensor_tensor(scale_terms[:, c, :, :], owner, spread(up_scale[:, 0:E, c], EA, 1), ALU.mult)
                then(last)
                for c in range(FC):
                    last = v.tensor_reduce(tile_scale[:, :, c], scale_terms[:, c, :, :], AX.X, ALU.add)
                then(last)

            def body(b, par, e):
                for u in units_of(b):
                    g = b * UNITS + u
                    if is_static(b) and b == B and u == HT_AT + 2:
                        dve.wait_ge(route_full, 1)
                        logits_out(B - 1, None, FB[0])
                        choose_experts()
                    if is_static(b) and b == B and u == 14:
                        count_tokens()
                    if is_static(b) and b == B + 1 and u == 1:
                        place_tokens()
                    if has_attention(b):
                        dve.wait_ge(scores_ready, g + 1)
                        v.tensor_reduce(neg_max[:, u % 4:u % 4 + 1], S[u % 2][:, :], AX.X, ALU.max, negate=True)\
                            .then_inc(max_ready, 1)
                    if has_tail(b) and u - 1 in TAIL_AT:
                        tail_dve(b, TAIL_AT[u - 1])
                    if has_down(b) and u == DOWN_AT + 1:
                        tail_dve(b - 1, DOWN)
                    if has_front(b) and u - 1 in FRONT_AT:
                        front_lo(b, par, FRONT_AT[u - 1])
                    if has_attention(b) and u == 0:
                        front_lo(b - 1, 1 - par, V1)
                    if (has_attention(b) and not (is_static(b) and b == 0 and u == 0)) or (is_static(b) and b == B and u == 0):
                        s = (u + 1) % 2
                        dve.wait_ge(pt_hi_ready, g)
                        v.tensor_tensor(pt_lo[s][:, :, :], PT[s][:, :].rearrange("p (k i) -> p k i", k=KB),
                                        pt_hi[s][:, :, :], ALU.subtract).then_inc(pt_lo_ready, 1)
                    if u % 4 == 1 and ((has_attention(b) and not (is_static(b) and b == 0 and u == 1)) or
                                       (is_static(b) and b == B and u == 1)):
                        normalise_heads(b * 4 + u // 4 - 1, (u // 4 - 1) % 4)
                    if has_front(b):
                        if u == 0:
                            stats_front(b)
                        if u == 1:
                            variance_front(b)
                        if is_static(b) and b <= 0:
                            prep_dve(b, u)
                        elif u in QUANTISE_AT:
                            quantise(matrix_of(b + 1), e, par == 0, QUANTISE_AT[u])
                    if has_tail(b):
                        if u - 1 in TAIL_AT:
                            residual_stats(b, TAIL_AT[u - 1])

            slots(dve, body)

            table()


            def split_lo(a, s):
                dve.wait_ge(e_ht_hi, a + 1)
                v.tensor_tensor(e_htl[s], e_htf[s], e_hth[s], ALU.subtract).then_inc(e_ht_lo, 1)

            def gate_up(a, s):
                dve.wait_ge(e_up_full, a + 1)
                sc = tile_scale[:, bass.ds(a, 1), :].rearrange("p a c -> p (a c)")
                v.tensor_tensor(e_up[s].rearrange("p (c t) -> p c t", c=FC),
                                PT[s][:, :].rearrange("p (c t) -> p c t", c=FC),
                                spread(sc, [P, FC, P], 2), ALU.mult).then_inc(e_u, 1)

            def through_gate(a, s):
                dve.wait_ge(e_th, a + 1)
                v.scalar_tensor_tensor(e_gate[s], e_tanh[s], 1.0, e_up[s], ALU.add, ALU.mult).then_inc(e_g, 1)

            def gate_lo(a, s):
                dve.wait_ge(e_g_hi, a + 1)
                v.tensor_tensor(e_gl[s], e_gate[s], e_gh[s], ALU.subtract).then_inc(e_g_lo, 1)

            def scale_out(a, s, e):
                dve.wait_ge(e_down_full, a + 1)
                if not (is_static(a) and a < 2):
                    dve.wait_ge(e_out, a - 1)
                v.scalar_tensor_tensor(e_yv[s], OE[s], slot_prob[:, bass.ds(a, 1)],
                                       row_scales[:, bass.ds(e, 1), :].rearrange("p a d -> p (a d)"),
                                       ALU.mult, ALU.mult).then_inc(e_y, 1)

            def step(k, r, n, expert):
                if isinstance(k, int) and k == 3:
                    dve.wait_ge(rowscale_free, 4)
                if tile_in_range(k - 3):
                    scale_out(k - 3, (r + 1) % 2, expert(3))
                if tile_in_range(k - 1):
                    through_gate(k - 1, (r + 1) % 2)
                if tile_in_range(k - 2):
                    expert(2)
                if tile_in_range(k):
                    gate_up(k, r % 2)
                if tile_in_range(k + 1):
                    split_lo(k + 1, (r + 1) % 2)
                if tile_in_range(k - 1):
                    gate_lo(k - 1, (r + 1) % 2)

            tiles(dve, step)

        @block.tensor
        def _(pe):
            mm = nc.tensor.matmul
            pe.wait_ge(const_ready, 9)

            def transpose_ternary(n, down, dst):
                pe.wait_ge(tern_ready, n + 1)
                for i in range(8):
                    outer, inner = (i // DC, i % DC) if down else (i // FC, i % FC)
                    cols = inner * FW + outer * P if down else inner * D + outer * P
                    last = nc.tensor.transpose(dst[:, i * P:(i + 1) * P], above[:, cols:cols + P], ident16[:, :])
                return last

            def prep_job(j):
                at_least(pe, prep_free, j)
                if j in (SHARED_UP, SHARED_DOWN):
                    last = transpose_ternary(2 if j == SHARED_DOWN else 0, j == SHARED_DOWN, tb16)
                elif j == ROUTER_W:
                    pe.wait_ge(rw_in, 16)
                    for c in range(DC):
                        last = nc.tensor.transpose(TBK[:, c * E:(c + 1) * E], rw_raw[:, c * P:(c + 1) * P],
                                                   ident[0:E, 0:E])
                elif j == BIAS:
                    pe.wait_ge(bo_in, 16)
                    last = mm(TBK[:, 0:D], ones[0:1, :], bo_raw, start=True, stop=True)
                else:
                    pe.wait_ge(diag_ready, DC)
                    last = mm(TBK[:, 0:D], ones[:, :], diag[:, :, :], start=True, stop=True)
                last.then_inc(prep_full, 1)

            def front_job(b, par, j):
                f, fp = b + 1, 1 - par
                k = (j + fp) % 2
                if is_static(f) and f == 0 and j in (V2, Q0, K0, V0):
                    pe.wait_ge(w_lo_ready, {V2: 1, Q0: 2, K0: 4, V0: 5}[j])
                if j == FC_CTX:
                    at_least(pe, tern_moved, f)
                    pe.wait_ge(c_loaded, (f + 1) * 16)
                elif j in (V2, Q0):
                    pe.wait_ge(f_lo, f * SPLIT + j)
                else:
                    pe.wait_ge(f_lo, f * SPLIT + j - 1)
                if j in (FC_CTX, FC_X):
                    if j == FC_X:
                        pe.wait_ge(x1_ready, f + 1)
                    src = c_in if j == FC_CTX else x1
                    for i in range(TB):
                        for c in range(DC):
                            last = nc.tensor.transpose(fb2[k][:, c, i * P:(i + 1) * P], src[:, i, c * P:(c + 1) * P],
                                                       ident[:, :])
                elif j in (V0, V1, V2, V3):
                    jb = {V0: 0, V1: 1, V2: 2, V3: 3}[j]
                    w = WV1 if jb < TB else WV2
                    cols = slice(jb * P, (jb + 1) * P)
                    last = split_product(FB[k][:, :], [(xt_hi[:, c, cols], xt_lo[:, c, cols], w_hi[:, w, c, :], w_lo[:, w, c, :])
                                                    for c in range(DC)])
                elif j in (Q0, Q1):
                    for n in range(2):
                        cols = slice((2 * (j - Q0) + n) * P, (2 * (j - Q0) + n + 1) * P)
                        last = split_product(fb2[k][:, n, :], [(w_hi[:, WQ, c, cols], w_lo[:, WQ, c, cols],
                                                             xt_hi[:, c, 0:T], xt_lo[:, c, 0:T]) for c in range(DC)])
                elif j == QUANT:
                    last = transpose_ternary(matrix_of(f), fp == 1, fb16[k])
                else:
                    cols = slice((j - K0) * P, (j - K0 + 1) * P)
                    for n, w in enumerate((WK1, WK2)):
                        last = split_product(fb2[k][:, n, :], [(w_hi[:, w, c, cols], w_lo[:, w, c, cols],
                                                                xt_hi[:, c, n * T:(n + 1) * T], xt_lo[:, c, n * T:(n + 1) * T])
                                                            for c in range(DC)])
                last.then_inc(f_full, 1)

            def scores(b, par, u):
                g = b * UNITS + u
                ib, h = u // HEADS, u % HEADS
                if u == 0:
                    for s in range(2):
                        pe.wait_ge(q_stacked[s], (b + 1) * 64)
                    for c in range(IC):
                        pe.wait_ge(k_stacked[c], (b + 1) * 64)
                if not (is_static(b) and b == 0 and u < 2):
                    pe.wait_ge(probs_ready, g - 1)
                for k in range(2):
                    last = mm(S[u % 2][:, :], q_st[par][:, h, k, ib * P:(ib + 1) * P], k_st[par][:, h, :],
                              start=(k == 0), stop=(k == 1))
                last.then_inc(scores_ready, 1)

            def transpose_probs(g, s, ring):
                pe.wait_ge(probs_ready, g + 1)
                if ring:
                    pe.wait_ge(pt_lo_ready, g - 1)
                for k in range(KB):
                    last = nc.tensor.transpose(PT[s][:, k * P:(k + 1) * P], probs[s][:, k * P:(k + 1) * P], ident[:, :])
                last.then_inc(pt_ready, 1)

            def weigh_values(g, u, par, group, ring):
                h = u % HEADS
                if u % 4 == 0 and ring:
                    pe.wait_ge(normed, group)
                pe.wait_ge(pt_lo_ready, g + 1)
                o1 = O[:, h * DH:(h + 1) * DH]
                for jb in range(KB):
                    mm(o1, pt_hi[u % 2][:, jb, :], v_st[par][:, 0, jb, h, :], start=(jb == 0), stop=False)
                    mm(o1, pt_hi[u % 2][:, jb, :], v_st[par][:, 1, jb, h, :], start=False, stop=False)
                    last = mm(o1, pt_lo[u % 2][:, jb, :], v_st[par][:, 0, jb, h, :], start=False, stop=(jb == KB - 1))
                last.then_inc(pv_done, 1)

            def ranks():
                pe.wait_ge(onehot_ready, 1)
                mm(S[0][:, 0:TILES * E], below16[:, :], hot16, start=True, stop=True)
                mm(S[1][:, 0:TILES * E], ones16[:, :], hot16, start=True, stop=True).then_inc(ranks_ready, 1)

            def route(src):
                for i in range(TB):
                    tok = slice(i * P, (i + 1) * P)
                    last = split_product(src[:, D + i * E:D + (i + 1) * E],
                                         [(ht_hi[:, c, tok], ht_lo[:, c, tok], rw_hi[:, c, :], rw_lo[:, c, :])
                                          for c in range(DC)])
                return last

            def tail_job(b, j):
                t = b - 1
                read, count = {OT0: (shared_ready, t), WO0: (ot_lo_ready, t * 2 + 1), OT1: (x2_ready, t * 2 + 1),
                               WO1: (ot_lo_ready, t * 2 + 2), HT: (x2_ready, t * 2 + 2),
                               UP0: (ht_ready, t + 1), UP1: (gate_ready, t * 2 + 1),
                               DOWN: (gate_ready, t * 2 + 2)}[j]
                at_least(pe, read, count)
                if j in (OT0, OT1):
                    i = int(j == OT1)
                    pe.wait_ge(normed, t * 4 + 2 * i + 2)
                    if i == 1:
                        at_least(pe, logits_ready, t)
                    elif is_static(t) and t == 0:
                        pe.wait_ge(prep_free, PREP)
                    for c in range(IC):
                        last = nc.tensor.transpose(TBK[:, c * P:(c + 1) * P], o_sb[:, i, c * P:(c + 1) * P], ident[:, :])
                elif j in (WO0, WO1):
                    if is_static(t) and t == 0 and j == WO0:
                        pe.wait_ge(w_lo_ready, 6)
                    last = split_product(TBK[:, 0:D], [(ot_hi[:, c, :], ot_lo[:, c, :], wo_hi[:, c, :], wo_lo[:, c, :])
                                                       for c in range(IC)])
                    if j == WO0 and not (is_static(t) and t == 0):
                        last = route(TBK)
                elif j == HT:
                    pe.wait_ge(hn_ready, t + 1)
                    for i in range(TB):
                        for c in range(DC):
                            last = nc.tensor.transpose(tb2[:, c, i * P:(i + 1) * P], row[:, i, D + c * P:D + (c + 1) * P],
                                                       ident[:, :])
                elif j in (UP0, UP1):
                    if j == UP0:
                        pe.wait_ge(h_lo_ready, t + 1)
                    for k in range(2):
                        n = 2 * (j - UP0) + k
                        for c in range(DC):
                            w = up16[:, E, c, n * P:(n + 1) * P]
                            mm(tb2[:, k, :], w, ht_hi[:, c, :], start=(c == 0), stop=False)
                            last = mm(tb2[:, k, :], w, ht_lo[:, c, :], start=False, stop=(c == DC - 1))
                else:
                    pe.wait_ge(g_lo_ready, t * 2 + 2)
                    for i in range(TB):
                        tok = slice(i * P, (i + 1) * P)
                        for c in range(FC):
                            mm(tb2[:, i, :], g_hi[:, c, tok], down16[:, E, c, :], start=(c == 0), stop=False)
                            last = mm(tb2[:, i, :], g_lo[:, c, tok], down16[:, E, c, :], start=False, stop=(c == FC - 1))
                last.then_inc(t_full, 1)

            def values(b, par, u):
                last = is_static(b) and b == B
                if (has_attention(b) and not (is_static(b) and b == 0 and u < 2)) or (last and u < 2):
                    g, pu = b * UNITS + u, (u - 2) % UNITS
                    pp = par if u >= 2 else 1 - par
                    weigh_values(g - 2, pu, pp, b * 4 + (u - 2) // 4, not (is_static(b) and g - 2 < 4))

            def body(b, par, e):
                last_slot = is_static(b) and b == B
                for u in units_of(b):
                    g = b * UNITS + u
                    if (has_attention(b) and not (is_static(b) and b == 0 and u == 0)) or (last_slot and u == 0):
                        transpose_probs(g - 1, (u + 1) % 2, not (is_static(b) and g - 1 < 2))
                    late = u % 4 == 2
                    if not late:
                        values(b, par, u)
                    if u + 1 < UNITS and has_attention(b):
                        scores(b, par, u + 1)
                    elif u + 1 == UNITS and (not is_static(b) or b + 1 < B):
                        scores(b + 1, 1 - par, 0)
                    if has_tail(b) and u in TAIL_AT:
                        tail_job(b, TAIL_AT[u])
                    if has_down(b) and u == DOWN_AT:
                        tail_job(b - 1, DOWN)
                    if is_static(b) and b == B and u == HT_AT + 1:
                        pe.wait_ge(h_lo_ready, B)
                        route(FB[0]).then_inc(route_full, 1)
                    if is_static(b) and b == B and u == 13:
                        ranks()
                    if is_static(b) and b <= 0 and u in PREP_AT[b]:
                        prep_job(PREP_AT[b][u])
                    if has_front(b) and u in FRONT_AT:
                        front_job(b, par, FRONT_AT[u])
                    if late:
                        values(b, par, u)

            slots(pe, body)

            pe.wait_ge(maps_ready, 4)
            for n, m in enumerate((map_ids, map_probs)):
                for i in range(TILES):
                    last = mm(TBK[:, n * 2 * SLOTS:(n + 1) * 2 * SLOTS].rearrange("p (g a) -> p g a", g=2),
                              lane_hot[:, i, :], m[:, i, :, :], start=(i == 0), stop=(i == TILES - 1))
            last.then_inc(slots_ready, 1)
            pe.wait_ge(dmat_ready, 1)
            for n in range(4):
                at_least(pe, rowscale_free, n)
                mm(FB[0][:, :], ones[:, :], diag_all[:, n * 512:(n + 1) * 512], start=True, stop=True)\
                    .then_inc(rowscale_full, 1)
            pe.wait_ge(table_ready, 1)

            def rows_to_columns(a, s, k, n):
                pe.wait_ge(gathered[k], (n + 1) * 16)
                if not (is_static(a) and a < 2):
                    pe.wait_ge(e_ht, a - 1)
                for c in range(DC):
                    last = nc.tensor.transpose(S[s][:, c * P:(c + 1) * P], g_rows[k][:, D + c * P:D + (c + 1) * P],
                                               ident[:, :])
                last.then_inc(e_ht_full, 1)

            def up(a, s, e):
                pe.wait_ge(e_ht_lo, a + 1)
                if not (is_static(a) and a < 2):
                    pe.wait_ge(e_u, a - 1)
                for n in range(FC):
                    for c in range(DC):
                        w = up16[:, bass.ds(e, 1), c, n * P:(n + 1) * P].rearrange("p a f -> p (a f)")
                        o1 = PT[s][:, n * P:(n + 1) * P]
                        mm(o1, w, e_hth[s][:, c, :], start=(c == 0), stop=False)
                        last = mm(o1, w, e_htl[s][:, c, :], start=False, stop=(c == DC - 1))
                last.then_inc(e_up_full, 1)

            def down(a, s, e):
                pe.wait_ge(e_g_lo, a + 1)
                if not (is_static(a) and a < 2):
                    pe.wait_ge(e_y, a - 1)
                for c in range(FC):
                    w = down16[:, bass.ds(e, 1), c, :].rearrange("p a d -> p (a d)")
                    mm(OE[s], e_gh[s][:, c * P:(c + 1) * P], w, start=(c == 0), stop=False)
                    last = mm(OE[s], e_gl[s][:, c * P:(c + 1) * P], w, start=False, stop=(c == FC - 1))
                last.then_inc(e_down_full, 1)

            def step(k, r, n, expert):
                if tile_in_range(k):
                    up(k, r % 2, expert(0))
                if tile_in_range(k + 2):
                    rows_to_columns(k + 2, r % 2, (r + 2) % RING, n + (r + 2) // RING)
                if tile_in_range(k - 2):
                    down(k - 2, r % 2, expert(2))

            tiles(pe, step)


_INS = ["x", "ctx_1024", "L0_xattn_Wq1", "L0_xattn_Wk1", "L0_xattn_Wv1", "L0_xattn_Wk2", "L0_xattn_Wv2",
        "L0_xattn_Wo", "L0_xattn_bo", "L0_ffn_shared_w1", "L0_ffn_shared_w2", "L0_ffn_expert_w1",
        "L0_ffn_expert_w2", "L0_ffn_router_w", "L0_ffn_ln_gamma", "L0_ffn_ln_beta"]


def kernel(**inputs):
    import numpy as np
    import concourse.bacc as bacc
    from concourse.bass_utils import run_bass_kernel_spmd

    nc = bacc.Bacc("TRN2", target_bir_lowering=False, num_devices=1)
    arrays, args = {}, []
    for name in _INS:
        a = np.ascontiguousarray(inputs[name])
        arrays[f"in_{name}"] = a
        args.append(nc.dram_tensor(f"in_{name}", a.shape, mybir.dt.from_np(a.dtype), kind="ExternalInput").ap())
    out = nc.dram_tensor("out", [B * T, D], F32, kind="ExternalOutput").ap()
    xattn_ffn(nc, *args, out)
    r = run_bass_kernel_spmd(nc, [arrays], core_ids=[0])
    return r.results[0]["out"].reshape(B, T, D)
```
